# Optimizing a Trainium2 kernel written in Bass

```python
import numpy as np
import jax
import jax.numpy as jnp

def _softmax(x, axis=-1):
    return jax.nn.softmax(x, axis=axis)

def _gelu(x):
    return jax.nn.gelu(x, approximate=True)

def _silu(x):
    return jax.nn.silu(x)

def _sigmoid(x):
    return jax.nn.sigmoid(x)

def _layernorm(x, axis=-1, eps=1e-05):
    m = jnp.mean(x, axis=axis, keepdims=True)
    v = jnp.var(x, axis=axis, keepdims=True)
    return (x - m) / jnp.sqrt(v + eps)

def _scatter_add(tgt, idx, src, axis=0):
    return tgt.at[idx].add(src)

def _segment_sum(src, seg, n):
    return jax.ops.segment_sum(src, seg, n)
kernel_name = 'mk_adj_resnorm_d4_adj_r2_585aa7'

def setup_inputs(seed: int=0):
    np.random.seed(seed)
    _w = jnp.asarray

    def _rec_inputs():
        import jax
        import jax.numpy as jnp
        _gk = jax.random.key(seed)
        x = -1.56e-05 + 0.05755 * jax.random.normal(jax.random.fold_in(_gk, 1), (128, 128, 128), jnp.float32)
        _a = jax.random.bernoulli(jax.random.fold_in(_gk, 2), 0.125, (128, 128, 128))
        _a = jnp.logical_or(_a, jnp.eye(128, dtype=bool))
        _af = _a.astype(jnp.float32)
        _af = _af * jax.random.uniform(jax.random.fold_in(_gk, 3), (128, 128, 128), jnp.float32, 0.05, 0.00012207)
        adj = _af
        _nm = jnp.ones((128, 128), dtype=bool)
        nodemask = jnp.where(_nm, 1.0, 0.0).astype(jnp.float32)
        return (x, adj, nodemask)
    x, adj, nodemask = _rec_inputs()

    def _L0_gnn_setup():
        import jax, jax.numpy as jnp
        import numpy as np
        C = 1.0
        SQRT_C = jnp.float32(np.sqrt(C))
        MIN_NORM = 1e-15
        BALL_EPS = 0.004

        def _norm(x):
            return jnp.clip(jnp.linalg.norm(x, axis=-1, keepdims=True), MIN_NORM, None)

        def _artanh(x):
            return jnp.arctanh(jnp.clip(x, -1 + 1e-07, 1 - 1e-07))

        def logmap0(x):
            n = _norm(x)
            return _artanh(SQRT_C * n) * x / (SQRT_C * n)

        def expmap0(u):
            n = _norm(u)
            return jnp.tanh(SQRT_C * n) * u / (SQRT_C * n)

        def project(x):
            n = _norm(x)
            maxnorm = (1.0 - BALL_EPS) / SQRT_C
            return jnp.where(n > maxnorm, x * (maxnorm / n), x)
        key = jax.random.key(seed)
        k1, k2 = jax.random.split(key)
        B, N, D = (2, 4096, 128)
        x = project(expmap0(0.1 * jax.random.normal(k1, (B, N, D), dtype=jnp.float32)))
        adj = jax.random.uniform(k2, (B, N, N), dtype=jnp.float32) / N
        return {'x': x, 'adj': adj}
    _L0_gnn_all = _L0_gnn_setup()
    _L0_gnn_in = {k: v for k, v in _L0_gnn_all.items() if k in ()}
    del _L0_gnn_all

    def _L1_gnn_setup():
        import jax, jax.numpy as jnp
        import numpy as np
        B, N, D, C, L = (64, 256, 128, 128, 5)
        EDGE_P = 0.02

        def _gru_cell(m, h, w_ih, w_hh, b_ih, b_hh):
            gi = m @ w_ih.T + b_ih
            gh = h @ w_hh.T + b_hh
            i_r, i_z, i_n = jnp.split(gi, 3, axis=-1)
            h_r, h_z, h_n = jnp.split(gh, 3, axis=-1)
            r = jax.nn.sigmoid(i_r + h_r)
            z = jax.nn.sigmoid(i_z + h_z)
            n = jnp.tanh(i_n + r * h_n)
            return (1.0 - z) * n + z * h
        key = jax.random.key(seed)
        ks = jax.random.split(key, 8)
        x = jax.random.normal(ks[0], (B, N, D), dtype=jnp.float32)
        adj = (jax.random.uniform(ks[1], (B, N, N)) < EDGE_P).astype(jnp.float32)
        mask = jnp.ones((B, N), dtype=jnp.float32)
        s = 1.0 / np.sqrt(C).astype(np.float32)
        weight = jax.random.uniform(ks[2], (L, C, C), minval=-s, maxval=s, dtype=jnp.float32)
        w_ih = jax.random.uniform(ks[3], (3 * C, C), minval=-s, maxval=s, dtype=jnp.float32)
        w_hh = jax.random.uniform(ks[4], (3 * C, C), minval=-s, maxval=s, dtype=jnp.float32)
        b_ih = jax.random.uniform(ks[5], (3 * C,), minval=-s, maxval=s, dtype=jnp.float32)
        b_hh = jax.random.uniform(ks[6], (3 * C,), minval=-s, maxval=s, dtype=jnp.float32)
        return dict(x=x, adj=adj, mask=mask, weight=weight, w_ih=w_ih, w_hh=w_hh, b_ih=b_ih, b_hh=b_hh)
    _L1_gnn_all = _L1_gnn_setup()
    _L1_gnn_in = {k: v for k, v in _L1_gnn_all.items() if k in ('weight', 'w_ih', 'w_hh', 'b_ih', 'b_hh')}
    del _L1_gnn_all

    def _L2_gnn_setup():
        import jax, jax.numpy as jnp
        import numpy as np
        key = jax.random.key(seed)
        k1, k2, k3, k4 = jax.random.split(key, 4)
        B, N, d_in, d_out = (8, 1024, 128, 128)
        x = jax.random.normal(k1, (B, N, d_in), dtype=jnp.float32)
        adj_hat = jax.random.uniform(k2, (B, N, N), dtype=jnp.float32)
        W = jax.random.normal(k3, (d_out, d_in), dtype=jnp.float32) * (1.0 / np.sqrt(d_in))
        b = jax.random.normal(k4, (d_out,), dtype=jnp.float32) * 0.01
        return {'x': x, 'adj_hat': adj_hat, 'W': W, 'b': b}
    _L2_gnn_all = _L2_gnn_setup()
    _L2_gnn_in = {k: v for k, v in _L2_gnn_all.items() if k in ('W', 'b')}
    del _L2_gnn_all

    def _L3_gnn_setup():
        import jax, jax.numpy as jnp
        import numpy as np
        B, K, H = (32, 512, 128)
        LN_EPS = 1e-05

        def layer_norm(x, gamma, beta):
            mu = jnp.mean(x, axis=-1, keepdims=True)
            var = jnp.mean(jnp.square(x - mu), axis=-1, keepdims=True)
            return (x - mu) * jax.lax.rsqrt(var + LN_EPS) * gamma + beta
        key = jax.random.key(seed)
        k1, k2, k3, k4 = jax.random.split(key, 4)
        x = jax.random.normal(k1, (B, K, H), dtype=jnp.float32)
        adj = jax.random.uniform(k2, (B, K, K), dtype=jnp.float32)
        s = 1.0 / np.sqrt(H)
        W_rel = jax.random.normal(k3, (H, H), dtype=jnp.float32) * s
        b_rel = jnp.zeros((H,), dtype=jnp.float32)
        W_root = jax.random.normal(k4, (H, H), dtype=jnp.float32) * s
        ln_gamma = jnp.ones((H,), dtype=jnp.float32)
        ln_beta = jnp.zeros((H,), dtype=jnp.float32)
        return {'x': x, 'adj': adj, 'W_rel': W_rel, 'b_rel': b_rel, 'W_root': W_root, 'ln_gamma': ln_gamma, 'ln_beta': ln_beta}
    _L3_gnn_all = _L3_gnn_setup()
    _L3_gnn_in = {k: v for k, v in _L3_gnn_all.items() if k in ('W_rel', 'b_rel', 'W_root', 'ln_gamma', 'ln_beta')}
    del _L3_gnn_all
    return {'x': x, 'adj': adj, 'nodemask': nodemask, 'L1_gnn_weight': _L1_gnn_in['weight'], 'L1_gnn_w_ih': _L1_gnn_in['w_ih'], 'L1_gnn_w_hh': _L1_gnn_in['w_hh'], 'L1_gnn_b_ih': _L1_gnn_in['b_ih'], 'L1_gnn_b_hh': _L1_gnn_in['b_hh'], 'L2_gnn_W': _L2_gnn_in['W'], 'L2_gnn_b': _L2_gnn_in['b'], 'L3_gnn_W_rel': _L3_gnn_in['W_rel'], 'L3_gnn_b_rel': _L3_gnn_in['b_rel'], 'L3_gnn_W_root': _L3_gnn_in['W_root'], 'L3_gnn_ln_gamma': _L3_gnn_in['ln_gamma'], 'L3_gnn_ln_beta': _L3_gnn_in['ln_beta']}

def reference(x, adj, nodemask, L1_gnn_weight, L1_gnn_w_ih, L1_gnn_w_hh, L1_gnn_b_ih, L1_gnn_b_hh, L2_gnn_W, L2_gnn_b, L3_gnn_W_rel, L3_gnn_b_rel, L3_gnn_W_root, L3_gnn_ln_gamma, L3_gnn_ln_beta):
    import jax
    import jax.numpy as jnp

    def _L0_gnn_ref(x, adj):
        import jax, jax.numpy as jnp
        import numpy as np
        C = 1.0
        SQRT_C = jnp.float32(np.sqrt(C))
        MIN_NORM = 1e-15
        BALL_EPS = 0.004

        def _norm(x):
            return jnp.clip(jnp.linalg.norm(x, axis=-1, keepdims=True), MIN_NORM, None)

        def _artanh(x):
            return jnp.arctanh(jnp.clip(x, -1 + 1e-07, 1 - 1e-07))

        def logmap0(x):
            n = _norm(x)
            return _artanh(SQRT_C * n) * x / (SQRT_C * n)

        def expmap0(u):
            n = _norm(u)
            return jnp.tanh(SQRT_C * n) * u / (SQRT_C * n)

        def project(x):
            n = _norm(x)
            maxnorm = (1.0 - BALL_EPS) / SQRT_C
            return jnp.where(n > maxnorm, x * (maxnorm / n), x)
        x_tangent = logmap0(x)
        support_t = jnp.einsum('bij,bjd->bid', adj, x_tangent)
        return project(expmap0(support_t))

    def _L1_gnn_ref(x, adj, mask, weight, w_ih, w_hh, b_ih, b_hh):
        import jax, jax.numpy as jnp
        import numpy as np
        B, N, D, C, L = (64, 256, 128, 128, 5)
        EDGE_P = 0.02

        def _gru_cell(m, h, w_ih, w_hh, b_ih, b_hh):
            gi = m @ w_ih.T + b_ih
            gh = h @ w_hh.T + b_hh
            i_r, i_z, i_n = jnp.split(gi, 3, axis=-1)
            h_r, h_z, h_n = jnp.split(gh, 3, axis=-1)
            r = jax.nn.sigmoid(i_r + h_r)
            z = jax.nn.sigmoid(i_z + h_z)
            n = jnp.tanh(i_n + r * h_n)
            return (1.0 - z) * n + z * h
        A = (adj != 0).astype(x.dtype)
        h = x
        for l in range(weight.shape[0]):
            m = jnp.einsum('bnd,de->bne', h, weight[l])
            agg = jnp.einsum('bij,bid->bjd', A, m)
            h = _gru_cell(agg, h, w_ih, w_hh, b_ih, b_hh)
        return h * mask[..., None]

    def _L2_gnn_ref(x, adj_hat, W, b):
        import jax, jax.numpy as jnp
        import numpy as np
        N = adj_hat.shape[1]
        diag = jnp.diagonal(adj_hat, axis1=-2, axis2=-1)
        d = adj_hat.sum(axis=-1) - diag
        d_inv_sqrt = jnp.power(d, -0.5)
        dad = d_inv_sqrt[:, :, None] * adj_hat * d_inv_sqrt[:, None, :]
        h = jnp.einsum('bnd,od->bno', x, W) + b
        return jnp.einsum('bnm,bmo->bno', dad, h)

    def _L3_gnn_ref(x, adj, W_rel, b_rel, W_root, ln_gamma, ln_beta):
        import jax, jax.numpy as jnp
        import numpy as np
        B, K, H = (32, 512, 128)
        LN_EPS = 1e-05

        def layer_norm(x, gamma, beta):
            mu = jnp.mean(x, axis=-1, keepdims=True)
            var = jnp.mean(jnp.square(x - mu), axis=-1, keepdims=True)
            return (x - mu) * jax.lax.rsqrt(var + LN_EPS) * gamma + beta
        h = layer_norm(x, ln_gamma, ln_beta)
        agg = jnp.einsum('bij,bjh->bih', adj, h)
        conv = jnp.einsum('bkh,ho->bko', agg, W_rel) + b_rel + jnp.einsum('bkh,ho->bko', h, W_root)
        return x + jax.nn.relu(conv)
    x = _layernorm(x + _L0_gnn_ref(x, adj), axis=-1)
    x = _layernorm(x + _L1_gnn_ref(x, adj, nodemask, L1_gnn_weight, L1_gnn_w_ih, L1_gnn_w_hh, L1_gnn_b_ih, L1_gnn_b_hh), axis=-1)
    x = _layernorm(x + _L2_gnn_ref(x, adj, L2_gnn_W, L2_gnn_b), axis=-1)
    x = _layernorm(x + _L3_gnn_ref(x, adj, L3_gnn_W_rel, L3_gnn_b_rel, L3_gnn_W_root, L3_gnn_ln_gamma, L3_gnn_ln_beta), axis=-1)
    return x

_drawn_inputs = setup_inputs


def setup_inputs(seed=0):
    import zlib

    import numpy as np

    out = dict(_drawn_inputs(seed))
    spreads = {'L3_gnn_b_rel': (0.0, 0.275), 'L3_gnn_ln_gamma': (1.0, 0.2), 'L3_gnn_ln_beta': (0.0, 0.1)}
    factors = {'L2_gnn_b': 5.985}
    for name, (base, spread) in spreads.items():
        noise = np.random.default_rng([zlib.crc32(name.encode()), seed]).standard_normal(out[name].shape)
        drawn = base * np.exp(spread * noise) if base else spread * noise
        out[name] = jnp.asarray(drawn.astype(out[name].dtype))
    for name, factor in factors.items():
        out[name] = (out[name] * factor).astype(out[name].dtype)
    return out
```

```python
from contextlib import ExitStack

import concourse.bass as bass
from concourse import mybir

F32 = mybir.dt.float32
F16 = mybir.dt.float16
I32 = mybir.dt.int32
ALU = mybir.AluOpType
ACT = mybir.ActivationFunctionType
AX = mybir.AxisListType

P = 128
C = 4
G = 4
W = C * P
BG = G * C

EPS = 1e-5
TINY_SQ = 1e-30
ATANH_MAX = 1.0 - 1e-7
BALL_MAX = 1.0 - 0.004
SERIES_BELOW = 0.25
SCALE_EXP = 8

PRE_IN, PRE_ART, PRE_XT, PRE_MM, PRE_BALL, PRE_V, PRE_LN, PRE_X1, PRE_X1T = 0, 4, 6, 7, 11, 12, 15, 16, 18
PRE_DINV = 10
POST_V2, POST_LN2, POST_X2, POST_X2T, POST_H, POST_Y = 0, 4, 5, 6, 6, 8
POST_LN3, POST_X3, POST_H3, POST_AGG, POST_CONV, POST_LN4, POST_OUT = 12, 13, 14, 15, 17, 21, 24

ART_STEPS = 22
BALL_STEPS = 5
LN_STEPS = 9
LN3_STEPS = 13


def build(nc, x, adj, nodemask, weight, w_ih, w_hh, b_ih, b_hh, w2, b2, w_rel, b_rel, w_root, gamma, beta, out):
    NB = x.shape[0] // BG
    L = weight.shape[0]
    S = L * G
    SN = S - G
    LOOP0, LOOP1 = 2, NB - 2

    with ExitStack() as ctx:
        def sb(name, shape, dt=F32):
            return ctx.enter_context(nc.sbuf_tensor(name, shape, dt))

        def pb(name, dt=F32):
            return ctx.enter_context(nc.psum_tensor(name, [P, 2048 // mybir.dt.size(dt)], dt))

        def sem(name):
            return ctx.enter_context(nc.semaphore(name))

        def sems(name, n):
            return [sem(f"{name}{i}") for i in range(n)]

        ident = sb("ident", [P, P])
        ident16 = sb("ident16", [P, P], F16)
        offdiag = sb("offdiag", [P, P])
        half16 = sb("half16", [P, 2, BG])
        w_hh_n = sb("w_hh_n", [P, 3, P])
        v_hi = sb("v_hi", [P, L, 3, P], F16)
        v_lo = sb("v_lo", [P, L, 3, P], F16)
        u_hi = sb("u_hi", [P, 3, P], F16)
        u_lo = sb("u_lo", [P, 3, P], F16)
        rowmax = sb("rowmax", [P, 3, 3])
        up = sb("up", [P, 3])
        down = sb("down", [P, 3])
        bi = sb("bi", [P, 3])
        bh = sb("bh", [P, 3])
        bias_rz = sb("bias_rz", [P, 3])
        bias_hn = sb("bias_hn", [P, 1])
        w2_n = sb("w2_n", [P, P])
        w2T = sb("w2T", [P, P])
        b2_row = sb("b2_row", [P, P])
        w_rel_s = sb("w_rel_s", [P, P])
        w_root_s = sb("w_root_s", [P, P])
        b_rel_row = sb("b_rel_row", [P, P])
        gamma_row = sb("gamma_row", [P, P])
        beta_row = sb("beta_row", [P, P])
        mask_n = sb("mask_n", [P, P])
        maskT = sb("maskT", [P, P])

        x_in = sb("x_in", [P, G, C, P])
        adj_in = sb("adj_in", [P, G, C, P])
        adj_off = sb("adj_off", [P, 2, C, P])
        adjT_pre = sb("adjT_pre", [P, G, C, P])
        x_tan = sb("x_tan", [P, 2, C, P])
        v1 = sb("v1", [P, G, C, P])
        x1_pre = sb("x1_pre", [P, G, C, P])
        act_junk = sb("act_junk", [P, C, P], F16)
        sumsq = sb("sumsq", [P, BG])
        art = sb("art", [P, 12, BG])
        tan_scale = sb("tan_scale", [P, BG])
        sup_sq = sb("sup_sq", [P, BG])
        ball = sb("ball", [P, 4, BG])
        degree = sb("degree", [P, BG])
        dinv_pre = sb("dinv_pre", [P, BG])
        dinv_mid = sb("dinv_mid", [P, BG])
        dinv_post = sb("dinv_post", [P, BG])
        st1, st2, st3, st4 = (sb(f"st{i}", [P, BG, 6]) for i in range(1, 5))
        ln1, ln2, ln4 = (sb(f"ln{i}", [P, 9, BG]) for i in (1, 2, 4))
        ln3 = sb("ln3", [P, 11, BG])

        linked = sb("linked", [P, G, W], F16)
        n_first = sb("n_first", [P, G, 2, C, P], F16)
        h_first = sb("h_first", [P, G, W])
        hh_first = sb("hh_first", [P, G, W], F16)
        hl_first = sb("hl_first", [P, G, W], F16)
        n_st = sb("n_st", [P, G, 2, C, P], F16)
        h_st = sb("h_st", [P, G, W])
        hh_st = sb("hh_st", [P, G, W], F16)
        hl_st = sb("hl_st", [P, G, W], F16)
        agg_hi = sb("agg_hi", [P, 2, W], F16)
        agg_lo = sb("agg_lo", [P, 2, W], F16)
        r_s = sb("r_s", [P, 2, W])
        z_s = sb("z_s", [P, 2, W])
        t_s = sb("t_s", [P, 2, W])
        c_s = sb("c_s", [P, 2, W])
        d_s = sb("d_s", [P, 2, W])

        adjT_mid = sb("adjT_mid", [P, G, C, P])
        adjT_post = sb("adjT_post", [P, G, C, P])
        x1_post = sb("x1_post", [P, G, C, P])
        mask_post = sb("mask_post", [P, BG])
        res = sb("res", [P, G, C, P])
        x2T = sb("x2T", [P, 2, W])
        h2 = sb("h2", [P, 2, C, P])
        h3 = sb("h3", [P, 2, C, P])
        h3T = sb("h3T", [P, 2, W])
        agg3 = sb("agg3", [P, 2, W])
        v4 = sb("v4", [P, G, C, P])

        res_flat = res[:, :, :, :].rearrange("p g c d -> p (g c d)")
        w_ih_n = res_flat[:, 0:3 * P].rearrange("p (k c) -> p k c", k=3)
        w_ihT = res_flat[:, 3 * P:6 * P].rearrange("p (k c) -> p k c", k=3)
        weight_n = res_flat[:, 6 * P:(6 + L) * P].rearrange("p (l c) -> p l c", l=L)
        weightT = res_flat[:, (6 + L) * P:(6 + 2 * L) * P]
        vT = v4[:, :, :, :].rearrange("p g c d -> p (g c d)")[:, 0:3 * L * P].rearrange("p (k c) -> p k c", k=3)

        p_hn, p_r, p_in, p_z, p_agg = (pb(f"p_{n}") for n in ("hn", "r", "in", "z", "agg"))
        p_nt = pb("p_nt", F16)
        p_a, p_b = pb("p_a"), pb("p_b")
        banks = {"a": p_a, "b": p_b}

        s_w = sems("s_w", 14)
        s_const = sem("s_const")
        s_set_pe = sem("s_set_pe")
        s_set_dve = sem("s_set_dve")
        s_half = sem("s_half")
        s_set_act = sem("s_set_act")
        x_loaded, adj_loaded = sems("x_loaded", G), sems("adj_loaded", G)
        adjT_mid_in, adjT_post_in, x1_post_in = sems("adjT_mid_in", G), sems("adjT_post_in", G), sems("x1_post_in", G)
        mask_in = sem("mask_in")
        out_stored = sems("out_stored", G)
        names = """sumsq_done adj_off_done degree_done adjT_ps adjT_ready art_step art_ln_done dinv_pre_done dinv_mid_done
            dinv_post_done x_tan_ready sup_ps sup_ready sup_sq_done ball_step v1_done st1_done ln1_step x1_ready
            n_first_hi n_first_lo x1T_ps h_first_ready hh_first_ready hl_first_ready linked_ready
            agg_ps agg_hi_ready agg_lo_ready gates_ps r_ready t_done t2_done cand_ready z_ready d_ready zd_done h_done
            hh_ready hl_ready nt_ps n_ready
            hT_ps v2_done st2_done ln2_step x2_ready x2T_ps x2T_ready h2_ps h2b_done h2s_ready y_ps v3_done st3_done
            ln3_step x3_ready h3g_done h3_ready h3T_ps agg3_ps h3T_ready agg3_ready conv_ps conv_done v4_done
            st4_done ln4_step out_ready""".split()
        (sumsq_done, adj_off_done, degree_done, adjT_ps, adjT_ready, art_step, art_ln_done, dinv_pre_done, dinv_mid_done,
         dinv_post_done, x_tan_ready, sup_ps, sup_ready, sup_sq_done, ball_step, v1_done, st1_done, ln1_step, x1_ready,
         n_first_hi, n_first_lo, x1T_ps, h_first_ready, hh_first_ready, hl_first_ready, linked_ready,
         agg_ps, agg_hi_ready, agg_lo_ready, gates_ps, r_ready, t_done, t2_done, cand_ready, z_ready, d_ready,
         zd_done, h_done, hh_ready, hl_ready, nt_ps, n_ready,
         hT_ps, v2_done, st2_done, ln2_step, x2_ready, x2T_ps, x2T_ready, h2_ps, h2b_done, h2s_ready, y_ps, v3_done,
         st3_done, ln3_step, x3_ready, h3g_done, h3_ready, h3T_ps, agg3_ps, h3T_ready, agg3_ready, conv_ps, conv_done,
         v4_done, st4_done, ln4_step, out_ready) = (sem(n) for n in names)

        def ge(eng, s, value):
            if not isinstance(value, int) or value > 0:
                eng.wait_ge(s, value)

        def live(batch):
            return not isinstance(batch, int) or 0 <= batch < NB

        def due(b, t, first, ahead):
            for g in range(G):
                if (first + g) % S == t:
                    batch = b + ahead - (first + g) // S
                    if live(batch):
                        yield batch, g

        def due_batch(b, t, first, ahead):
            batch = b + ahead - first // S
            return [batch] if first % S == t and live(batch) else []

        def earlier(b, t, back):
            batch, slot = (b, t - back) if t >= back else (b - 1, t - back + S)
            return [(batch, slot)] if live(batch) else []

        def following(b, t):
            batch, slot = (b, t + 1) if t < S - 1 else (b + 1, 0)
            return [(batch, slot)] if live(batch) else []

        def run(eng, slot):
            for b in range(-1, LOOP0):
                for t in range(S):
                    slot(b, t)
            with eng.Fori(LOOP0, LOOP1) as b:
                for t in range(S):
                    slot(b, t)
            for b in range(LOOP1, NB + 2):
                for t in range(S):
                    slot(b, t)

        def graphs(row):
            return row[:, :].unsqueeze(1).broadcast_to([P, C, P])

        def columns(small, g):
            return small[:, C * g:C * g + C].unsqueeze(2).broadcast_to([P, C, P])

        def col(small, g, c):
            return small[:, C * g + c:C * g + c + 1]

        RSTD, SHIFT, VAR = 6, 7, 5

        def ln_dve(dve, st, ln, step, steps, batch, st_done, eps=EPS):
            me, mo, qe, qo = st[:, :, 1], st[:, :, 4], st[:, :, 2], st[:, :, 5]
            ge(dve, st_done, G * batch + G)
            dve.tensor_tensor(ln[:, 0], me, mo, ALU.add).then_inc(step, 1)
            dve.tensor_tensor(ln[:, 1], me, mo, ALU.subtract).then_inc(step, 1)
            dve.tensor_tensor(ln[:, 2], qe, qo, ALU.add).then_inc(step, 1)
            ge(dve, step, steps * batch + 2)
            dve.tensor_tensor(ln[:, 3], ln[:, 1], ln[:, 1], ALU.mult).then_inc(step, 1)
            ge(dve, step, steps * batch + 4)
            dve.scalar_tensor_tensor(out=ln[:, 4], in0=ln[:, 3], scalar=P / 4.0, in1=ln[:, 2],
                                     op0=ALU.mult, op1=ALU.add).then_inc(step, 1)
            ge(dve, step, steps * batch + 5)
            dve.tensor_scalar(ln[:, VAR], ln[:, 4], 1.0 / P, None, ALU.mult).then_inc(step, 1)
            ge(dve, step, steps * batch + 6)
            dve.tensor_scalar(ln[:, 8], ln[:, VAR], eps, None, ALU.add).then_inc(step, 1)

        def ln_pool(pool, ln, step, steps, batch, after=7):
            ge(pool, step, steps * batch + after)
            pool.tensor_tensor(ln[:, RSTD], ln[:, 8], half16[:, 1], ALU.pow).then_inc(step, 1)

        def ln_shift(dve, ln, step, steps, batch):
            ge(dve, step, steps * batch + steps - 1)
            dve.scalar_tensor_tensor(out=ln[:, SHIFT], in0=ln[:, 0], scalar=-0.5, in1=ln[:, RSTD],
                                     op0=ALU.mult, op1=ALU.mult).then_inc(step, 1)

        SET_MASK, SET_W2, SET_V = 4, 5, 9

        block = ctx.enter_context(nc.Block())

        @block.sync
        def _(sp):
            def load_x(at, g):
                src = x[bass.ds(at, C), :, :].rearrange("c n d -> n c d")
                sp.dma_start(x_in[:, g], src).then_inc(x_loaded[g], 16)

            def load_adj(at, g):
                src = adj[bass.ds(at, C), :, :].rearrange("c i j -> i c j")
                sp.dma_start(adj_in[:, g], src).then_inc(adj_loaded[g], 16)

            for g in range(G):
                load_x(C * g, g)
                load_adj(C * g, g)
            loads = [
                (w_ih_n[:, :, :], w_ih.rearrange("(k p) c -> p k c", p=P)),
                (weight_n[:, :, :], weight.rearrange("l d c -> d l c")),
                (w_hh_n[:, :, :], w_hh.rearrange("(k p) c -> p k c", p=P)),
                (bi[:, :], b_ih.rearrange("(k p) -> p k", p=P)),
                (bh[:, :], b_hh.rearrange("(k p) -> p k", p=P)),
                (mask_n[:, :], nodemask),
                (w2_n[:, :], w2),
                (b2_row[:, :], b2.partition_broadcast(P)),
                (w_rel_s[:, :], w_rel),
                (w_root_s[:, :], w_root),
                (b_rel_row[:, :], b_rel.partition_broadcast(P)),
                (gamma_row[:, :], gamma.partition_broadcast(P)),
                (beta_row[:, :], beta.partition_broadcast(P)),
            ]
            for (dst, src), s in zip(loads, s_w):
                sp.dma_start(dst, src, allow_slow_non_contiguous=True).then_inc(s, 16)

            def counts(*values):
                return [v if isinstance(v, int) else sp.compute_val(v) for v in values]

            def slot(b, t):
                for q, g in due(b, t, POST_OUT, -1):
                    at, rows = counts(q * BG + C * g, G * q + g + 1)
                    ge(sp, out_ready, rows)
                    dst = out[bass.ds(at, C), :, :].rearrange("c n d -> n c d")
                    sp.dma_start(dst, v4[:, g]).then_inc(out_stored[g], 16)
                if t == 5 and live(b):
                    at, read = counts(b * BG, G * b)
                    ge(sp, s_set_act, SET_MASK)
                    ge(sp, v2_done, read)
                    sp.dma_start(mask_post[:, :], maskT[:, bass.ds(at, BG)]).then_inc(mask_in, 16)
                    for g in range(G):
                        x1_there, = counts(G * b + g + 1)
                        ge(sp, x1_ready, x1_there)
                        sp.dma_start(x1_post[:, g], x1_pre[:, g]).then_inc(x1_post_in[g], 16)
                if t >= S - G - 1 and t < S - 1 and live(b + 2):
                    g = t - (S - G - 1)
                    at, read = counts((b + 2) * BG + C * g, G * (b + 1) + g + 1)
                    ge(sp, v1_done, read)
                    load_x(at, g)
                if t >= S - G:
                    g = t - (S - G)
                    if live(b + 2):
                        at, read = counts((b + 2) * BG + C * g, G * (b + 1) + g + 1)
                        ge(sp, linked_ready, read)
                        load_adj(at, g)
                    if live(b):
                        read, there = counts(G * (b - 1) + g + 1, 16 * (b + 1))
                        ge(sp, agg3_ps, read)
                        ge(sp, adjT_mid_in[g], there)
                        sp.dma_start(adjT_post[:, g], adjT_mid[:, g]).then_inc(adjT_post_in[g], 16)
                    if live(b + 1):
                        moved, there = counts(16 * (b + 1), G * (b + 1) + g + 1)
                        ge(sp, adjT_post_in[g], moved)
                        ge(sp, adjT_ready, there)
                        sp.dma_start(adjT_mid[:, g], adjT_pre[:, g]).then_inc(adjT_mid_in[g], 16)
            run(sp, slot)
            for g in range(G):
                sp.wait_ge(out_stored[g], 16 * NB)

        @block.gpsimd
        def _(pool):
            pool.memset(ident[:, :], 0.0).then_inc(s_const, 1)
            pool.memset(ident16[:, :], 0.0).then_inc(s_const, 1)
            pool.memset(offdiag[:, :], 1.0).then_inc(s_const, 1)
            pool.memset(half16[:, 0], 0.5).then_inc(s_const, 1)
            pool.memset(half16[:, 1], -0.5).then_inc(s_const, 1)
            pool.wait_ge(s_const, 5)
            for tile, fill in ((ident, 1.0), (ident16, 1.0), (offdiag, 0.0)):
                pool.affine_select(out=tile[:, :], in_=tile[:, :], compare_op=ALU.not_equal, fill=fill, base=0,
                                   pattern=[[-1, P]], channel_multiplier=1).then_inc(s_const, 1)
            pool.wait_ge(s_const, 8)

            def slot(b, t):
                for m, u in earlier(b, t, 2):
                    if u < SN:
                        ge(pool, hh_ready, SN * m + u + 1)
                        pool.tensor_tensor(hl_st[:, u % G], h_st[:, u % G], hh_st[:, u % G], ALU.subtract)\
                            .then_inc(hl_ready, 1)
                for m, u in earlier(b, t, 1):
                    h_old = h_first if u < G else h_st
                    ge(pool, cand_ready, S * m + u + 1)
                    pool.tensor_tensor(d_s[:, u % 2], h_old[:, u % G], c_s[:, u % 2], ALU.subtract).then_inc(d_ready, 1)
                for q, g in due(b, t, POST_H, -1):
                    ge(pool, dinv_post_done, q + 1)
                    ge(pool, h2b_done, G * q + g + 1)
                    pool.tensor_tensor(h2[:, g % 2], h2[:, g % 2], columns(dinv_post, g), ALU.mult)\
                        .then_inc(h2s_ready, 1)
                for q in due_batch(b, t, POST_LN2 + 1, -1):
                    ln_pool(pool, ln2, ln2_step, LN_STEPS, q)
                for q in due_batch(b, t, POST_LN3 + 1, -1):
                    pool.tensor_tensor(ln3[:, 10], ln3[:, 9], half16[:, 1], ALU.pow).then_inc(ln3_step, 1)
                for q in due_batch(b, t, POST_LN4 + 1, -1):
                    ln_pool(pool, ln4, ln4_step, LN_STEPS, q)
                for p in due_batch(b, t, PRE_LN + 1, 1):
                    ln_pool(pool, ln1, ln1_step, LN_STEPS, p)
                for p in due_batch(b, t, PRE_DINV, 1):
                    ge(pool, degree_done, G * p + G)
                    ge(pool, dinv_mid_done, p)
                    pool.tensor_tensor(dinv_pre[:, :], degree[:, :], half16[:, 1], ALU.pow).then_inc(dinv_pre_done, 1)
                for p, g in due(b, t, PRE_X1 + 1, 1):
                    ge(pool, n_first_hi, G * p + g + 1)
                    pool.tensor_tensor(n_first[:, g, 1], x1_pre[:, g], n_first[:, g, 0], ALU.subtract)\
                        .then_inc(n_first_lo, 1)
                for p, g in due(b, t, PRE_X1T, 1):
                    ge(pool, hh_first_ready, G * p + g + 1)
                    pool.tensor_tensor(hl_first[:, g], h_first[:, g], hh_first[:, g], ALU.subtract)\
                        .then_inc(hl_first_ready, 1)
                for p, g in due(b, t, PRE_IN, 1):
                    ge(pool, adj_loaded[g], 16 * (p + 1))
                    ge(pool, degree_done, G * p + g - 1)
                    pool.tensor_tensor(adj_off[:, g % 2], adj_in[:, g], graphs(offdiag), ALU.mult)\
                        .then_inc(adj_off_done, 1)
                for p, g in due(b, t, PRE_XT, 1):
                    ge(pool, art_step, ART_STEPS * (p + 1))
                    ge(pool, sup_ps, G * p + g - 1)
                    pool.tensor_tensor(x_tan[:, g % 2], x_in[:, g], columns(tan_scale, g), ALU.mult)\
                        .then_inc(x_tan_ready, 1)
                for q, g in due(b, t, POST_H3, -1):
                    ge(pool, h3g_done, G * q + g + 1)
                    pool.tensor_tensor(h3[:, g % 2], h3[:, g % 2], graphs(beta_row), ALU.add).then_inc(h3_ready, 1)
                for p in due_batch(b, t, PRE_ART, 1):
                    ge(pool, art_step, ART_STEPS * p + 1)
                    pool.tensor_tensor(art[:, 1], art[:, 0], half16[:, 0], ALU.pow).then_inc(art_step, 1)
                for p in due_batch(b, t, PRE_BALL, 1):
                    ge(pool, ball_step, BALL_STEPS * p + 1)
                    pool.tensor_tensor(ball[:, 1], ball[:, 0], half16[:, 0], ALU.pow).then_inc(ball_step, 1)
                for q in due_batch(b, t, POST_LN3, -1):
                    ln_pool(pool, ln3, ln3_step, LN3_STEPS, q, 10)
            run(pool, slot)

        @block.scalar
        def _(act):
            act.wait_ge(s_set_pe, 1)
            act.activation(w_ihT[:, :, :].rearrange("p k c -> p (k c)"), p_hn[:, 0:3 * P], ACT.Copy).then_inc(s_set_act, 1)
            act.wait_ge(s_set_pe, 2)
            act.activation(weightT[:, 0:W], p_r[:, :], ACT.Copy).then_inc(s_set_act, 1)
            act.wait_ge(s_set_pe, 3)
            act.activation(weightT[:, W:L * P], p_in[:, 0:L * P - W], ACT.Copy).then_inc(s_set_act, 1)
            act.wait_ge(s_set_pe, 4)
            act.activation(maskT[:, :], p_z[:, 0:P], ACT.Copy).then_inc(s_set_act, 1)
            act.wait_ge(s_set_pe, 5)
            act.activation(w2T[:, :], p_z[:, P:2 * P], ACT.Copy).then_inc(s_set_act, 1)
            for k in range(3):
                act.wait_ge(s_set_pe, 6 + k)
                act.activation(vT[:, k, 0:W], (p_hn, p_r, p_in)[k][:, :], ACT.Copy).then_inc(s_set_act, 1)
            act.wait_ge(s_set_pe, 9)
            act.activation(vT[:, :, W:L * P], p_agg[:, 0:3 * P].rearrange("p (k c) -> p k c", k=3), ACT.Copy)\
                .then_inc(s_set_act, 1)
            for l in range(L + 1):
                act.wait_ge(s_set_pe, 10 + l)
                hi = v_hi[:, l] if l < L else u_hi[:, :, :]
                act.activation(hi, (p_a, p_b)[l % 2][:, 0:3 * P].rearrange("p (k c) -> p k c", k=3), ACT.Copy)\
                    .then_inc(s_set_act, 1)

            def apply(dst, src, ln, g, done):
                for c in range(C):
                    last = act.activation(dst[:, g, c], src[:, g, c], ACT.Identity, bias=col(ln[:, SHIFT], g, c),
                                          scale=col(ln[:, RSTD], g, c))
                last.then_inc(done, 1)

            def slot(b, t):
                for p in due_batch(b, t, PRE_BALL + 1, 1):
                    ge(act, ball_step, BALL_STEPS * p + 2)
                    act.activation(ball[:, 2], ball[:, 1], ACT.Tanh).then_inc(ball_step, 1)
                if live(b):
                    ge(act, gates_ps, 4 * (S * b + t) + 2)
                    act.activation(r_s[:, t % 2], p_r[:, :], ACT.Sigmoid, bias=bias_rz[:, 0:1], scale=down[:, 0:1])\
                        .then_inc(r_ready, 1)
                for m, u in following(b, t):
                    ge(act, agg_ps, S * m + u + 1)
                    act.activation(agg_hi[:, u % 2], p_agg[:, :], ACT.Copy).then_inc(agg_hi_ready, 1)
                for p, g in due(b, t, PRE_X1T, 1):
                    ge(act, x1T_ps, G * p + g + 1)
                    act.activation(h_first[:, g], p_a[:, :], ACT.Copy).then_inc(h_first_ready, 1)
                    act.activation(hh_first[:, g], p_a[:, :], ACT.Copy).then_inc(hh_first_ready, 1)
                for p, g in due(b, t, PRE_MM, 1):
                    ge(act, sup_ps, G * p + g + 1)
                    act.activation(v1[:, g], p_a[:, :].rearrange("p (c d) -> p c d", c=C), ACT.Copy)\
                        .then_inc(sup_ready, 1)
                for q, g in due(b, t, POST_X2T, -1):
                    ge(act, x2T_ps, G * q + g + 1)
                    ge(act, h2_ps, G * q + g - 1)
                    act.activation(x2T[:, g % 2], p_b[:, :], ACT.Copy).then_inc(x2T_ready, 1)
                if live(b):
                    ge(act, gates_ps, 4 * (S * b + t) + 4)
                    ge(act, zd_done, S * b + t - 1)
                    act.activation(z_s[:, t % 2], p_z[:, :], ACT.Sigmoid, bias=bias_rz[:, 1:2], scale=down[:, 1:2])\
                        .then_inc(z_ready, 1)
                    ge(act, t2_done, S * b + t + 1)
                    ge(act, h_done, S * b + t - 1)
                    act.activation(c_s[:, t % 2], t_s[:, t % 2], ACT.Tanh, bias=bi[:, 2:3], scale=down[:, 2:3])\
                        .then_inc(cand_ready, 1)
                for m, u in earlier(b, t, 1):
                    if u < SN:
                        ge(act, h_done, S * m + u + 1)
                        act.activation(hh_st[:, u % G], h_st[:, u % G], ACT.Copy).then_inc(hh_ready, 1)
                for p, g in due(b, t, PRE_X1, 1):
                    ge(act, ln1_step, LN_STEPS * (p + 1))
                    ge(act, x1_post_in[g], 16 * p)
                    apply(x1_pre, v1, ln1, g, x1_ready)
                    ge(act, x1_ready, G * p + g + 1)
                    act.activation(n_first[:, g, 0], x1_pre[:, g], ACT.Copy).then_inc(n_first_hi, 1)
                for p, g in due(b, t, PRE_IN, 1):
                    ge(act, adjT_ps, G * p + g + 1)
                    ge(act, adjT_mid_in[g], 16 * p)
                    act.activation(adjT_pre[:, g].rearrange("p c i -> p (c i)"), p_a[:, :], ACT.Copy)\
                        .then_inc(adjT_ready, 1)
                for q, g in due(b, t, POST_AGG, -1):
                    ge(act, h3T_ps, G * q + g + 1)
                    ge(act, conv_ps, G * q + g - 1)
                    act.activation(h3T[:, g % 2], p_a[:, :], ACT.Copy).then_inc(h3T_ready, 1)
                    ge(act, agg3_ps, G * q + g + 1)
                    act.activation(agg3[:, g % 2], p_b[:, :], ACT.Copy).then_inc(agg3_ready, 1)
                for p in due_batch(b, t, PRE_ART + 1, 1):
                    ge(act, art_step, ART_STEPS * p + 7)
                    act.activation(art[:, 8], art[:, 7], ACT.Ln).then_inc(art_ln_done, 1)
                for q, g in due(b, t, POST_X2, -1):
                    ge(act, ln2_step, LN_STEPS * (q + 1))
                    apply(res, res, ln2, g, x2_ready)
                for q, g in due(b, t, POST_X3, -1):
                    ge(act, ln3_step, LN3_STEPS * (q + 1))
                    apply(res, res, ln3, g, x3_ready)
                for p, g in due(b, t, PRE_IN, 1):
                    ge(act, x_loaded[g], 16 * (p + 1))
                    ge(act, sumsq_done, G * p + g)
                    for c in range(C):
                        last = act.activation(act_junk[:, c], x_in[:, g, c], ACT.Square, accum_out=col(sumsq, g, c))
                    last.then_inc(sumsq_done, 1)
                for p, g in due(b, t, PRE_MM, 1):
                    ge(act, sup_ready, G * p + g + 1)
                    ge(act, sup_sq_done, G * p + g)
                    for c in range(C):
                        last = act.activation(act_junk[:, c], v1[:, g, c], ACT.Square, accum_out=col(sup_sq, g, c))
                    last.then_inc(sup_sq_done, 1)
            run(act, slot)

        @block.vector
        def _(dve):
            dve.wait_ge(s_w[2], 16)
            dve.tensor_reduce(rowmax[:, :, 0], w_hh_n[:, :, :], AX.X, ALU.max, apply_absolute_value=True)\
                .then_inc(s_set_dve, 1)
            dve.wait_ge(s_set_act, SET_V)
            dve.tensor_reduce(rowmax[:, :, 1], vT[:, :, :], AX.X, ALU.max, apply_absolute_value=True)\
                .then_inc(s_set_dve, 1)
            dve.wait_ge(s_set_dve, 2)
            dve.tensor_tensor(rowmax[:, :, 2], rowmax[:, :, 0], rowmax[:, :, 1], ALU.max).then_inc(s_set_dve, 1)
            dve.wait_ge(s_set_dve, 3)
            dve.tensor_scalar(up[:, :], rowmax[:, :, 2], 2.0 ** -100, 2.0 ** 100, ALU.max, ALU.min).then_inc(s_set_dve, 1)
            dve.wait_ge(s_set_dve, 4)
            down_i, up_i = down[:, :].bitcast(I32), up[:, :].bitcast(I32)
            dve.tensor_scalar(down_i, up_i, 0x7F800000, None, ALU.bitwise_and).then_inc(s_set_dve, 1)
            dve.wait_ge(s_set_dve, 5)
            dve.tensor_scalar(up_i, down_i, -1.0, float((254 + SCALE_EXP) << 23), ALU.mult, ALU.add).then_inc(s_set_dve, 1)
            dve.wait_ge(s_set_dve, 6)
            dve.tensor_scalar(down_i, up_i, -1.0, float(254 << 23), ALU.mult, ALU.add).then_inc(s_set_dve, 1)
            for k in range(3):
                dve.tensor_scalar(vT[:, k], vT[:, k], up[:, k:k + 1], None, ALU.mult).then_inc(s_set_dve, 1)
                dve.tensor_scalar(w_hh_n[:, k], w_hh_n[:, k], up[:, k:k + 1], None, ALU.mult).then_inc(s_set_dve, 1)
            dve.wait_ge(s_w[3], 16)
            dve.wait_ge(s_w[4], 16)
            dve.tensor_tensor(bias_rz[:, :], bi[:, :], bh[:, :], ALU.add).then_inc(s_set_dve, 1)
            dve.tensor_tensor(bias_hn[:, :], bh[:, 2:3], up[:, 2:3], ALU.mult).then_inc(s_set_dve, 1)
            for k, tile in ((8, w_rel_s), (9, w_root_s), (10, b_rel_row)):
                dve.wait_ge(s_w[k], 16)
                dve.tensor_scalar(tile[:, :], tile[:, :], 0.5, None, ALU.mult).then_inc(s_half, 1)
            for l in range(L + 1):
                dve.wait_ge(s_set_act, 10 + l)
                hi, lo = (v_hi[:, l], v_lo[:, l]) if l < L else (u_hi[:, :, :], u_lo[:, :, :])
                dve.tensor_tensor(lo, (p_a, p_b)[l % 2][:, 0:3 * P].rearrange("p (k c) -> p k c", k=3), hi, ALU.subtract)\
                    .then_inc(s_set_dve, 1)

            def bn(src, g, st, done, src_done, value):
                ge(dve, src_done, value)
                for c in range(C):
                    last = dve.bn_stats(st[:, C * g + c], src[:, g, c])
                last.then_inc(done, 1)

            def art_steps(p):
                k0 = ART_STEPS * p

                def ts(dst, src, wait, a, c_, oa, ob=ALU.bypass):
                    ge(dve, art_step, k0 + wait)
                    dve.tensor_scalar(dst, src, a, c_, oa, ob).then_inc(art_step, 1)

                def tt(dst, i0, i1, wait, op):
                    ge(dve, art_step, k0 + wait)
                    dve.tensor_tensor(dst, i0, i1, op).then_inc(art_step, 1)
                return k0, ts, tt

            def slot(b, t):
                n = S * b + t
                for p in due_batch(b, t, PRE_ART + 2, 1):
                    k0, ts, tt = art_steps(p)
                    ge(dve, art_ln_done, p + 1)
                    ge(dve, art_step, k0 + 18)
                    dve.scalar_tensor_tensor(out=art[:, 9], in0=art[:, 8], scalar=0.5, in1=art[:, 6],
                                             op0=ALU.mult, op1=ALU.mult).then_inc(art_step, 1)
                    tt(art[:, 11], art[:, 5], art[:, 9], 19, ALU.subtract)
                    tt(art[:, 11], art[:, 11], art[:, 10], 20, ALU.mult)
                    tt(tan_scale[:, :], art[:, 11], art[:, 9], 21, ALU.add)
                if live(b):
                    ge(dve, r_ready, n + 1)
                    dve.scalar_tensor_tensor(out=t_s[:, t % 2], in0=p_hn[:, :], scalar=bias_hn[:, 0:1],
                                             in1=r_s[:, t % 2], op0=ALU.add, op1=ALU.mult).then_inc(t_done, 1)
                for m, u in following(b, t):
                    ge(dve, agg_hi_ready, S * m + u + 1)
                    dve.tensor_tensor(agg_lo[:, u % 2], p_agg[:, :], agg_hi[:, u % 2], ALU.subtract)\
                        .then_inc(agg_lo_ready, 1)
                if live(b):
                    ge(dve, gates_ps, 4 * n + 3)
                    ge(dve, t_done, n + 1)
                    dve.tensor_tensor(t_s[:, t % 2], p_in[:, :], t_s[:, t % 2], ALU.add).then_inc(t2_done, 1)
                for q, g in due(b, t, POST_CONV, -1):
                    ge(dve, conv_ps, G * q + g + 1)
                    ge(dve, out_stored[g], 16 * q)
                    dve.tensor_tensor(v4[:, g], p_b[:, :].rearrange("p (c d) -> p c d", c=C), graphs(b_rel_row),
                                      ALU.add).then_inc(conv_done, 1)
                for m, u in earlier(b, t, 1):
                    ge(dve, z_ready, S * m + u + 1)
                    ge(dve, d_ready, S * m + u + 1)
                    dve.tensor_tensor(d_s[:, u % 2], z_s[:, u % 2], d_s[:, u % 2], ALU.mult).then_inc(zd_done, 1)
                    ge(dve, zd_done, S * m + u + 1)
                    if u < G:
                        ge(dve, hT_ps, G * (m - 1) + u + 1)
                    dve.tensor_tensor(h_st[:, u % G], c_s[:, u % 2], d_s[:, u % 2], ALU.add).then_inc(h_done, 1)
                if live(b) and 2 <= t < SN + 2:
                    u = t - 2
                    ge(dve, nt_ps, SN * b + u + 1)
                    dve.tensor_copy(n_st[:, u % G].rearrange("p s c d -> p (s c d)"), p_nt[:, :]).then_inc(n_ready, 1)
                for q, g in due(b, t, POST_CONV, -1):
                    ge(dve, conv_done, G * q + g + 1)
                    dve.scalar_tensor_tensor(out=v4[:, g], in0=v4[:, g], scalar=0.0, in1=res[:, g],
                                             op0=ALU.max, op1=ALU.add).then_inc(v4_done, 1)
                    bn(v4, g, st4, st4_done, v4_done, G * q + g + 1)
                for q, g in due(b, t, POST_H, -1):
                    ge(dve, h2_ps, G * q + g + 1)
                    ge(dve, y_ps, G * q + g - 1)
                    dve.tensor_tensor(h2[:, g % 2], p_b[:, :].rearrange("p (c d) -> p c d", c=C), graphs(b2_row), ALU.add)\
                        .then_inc(h2b_done, 1)
                for q in due_batch(b, t, POST_LN2 + 1, -1):
                    ln_shift(dve, ln2, ln2_step, LN_STEPS, q)
                for q in due_batch(b, t, POST_LN4 + 1, -1):
                    ln_shift(dve, ln4, ln4_step, LN_STEPS, q)
                for p in due_batch(b, t, PRE_LN + 1, 1):
                    ln_shift(dve, ln1, ln1_step, LN_STEPS, p)
                for q in due_batch(b, t, POST_LN3 + 1, -1):
                    ln_shift(dve, ln3, ln3_step, LN3_STEPS, q)
                for p in due_batch(b, t, PRE_ART + 1, 1):
                    k0, ts, tt = art_steps(p)
                    ts(art[:, 2], art[:, 1], 2, ATANH_MAX, None, ALU.min)
                    ts(art[:, 3], art[:, 2], 3, 1.0, None, ALU.add)
                    ts(art[:, 4], art[:, 2], 4, -1.0, 1.0, ALU.mult, ALU.add)
                    ge(dve, art_step, k0 + 5)
                    dve.reciprocal(art[:, 5], art[:, 4]).then_inc(art_step, 1)
                    tt(art[:, 7], art[:, 3], art[:, 5], 6, ALU.mult)
                    ge(dve, art_step, k0 + 7)
                    dve.reciprocal(art[:, 6], art[:, 1]).then_inc(art_step, 1)
                    tt(art[:, 3], art[:, 2], art[:, 2], 8, ALU.mult)
                    ts(art[:, 4], art[:, 3], 9, 1.0 / 15, None, ALU.mult)
                    for i, k in enumerate((13, 11, 9, 7, 5, 3)):
                        ge(dve, art_step, k0 + 10 + i)
                        dve.scalar_tensor_tensor(out=art[:, 4], in0=art[:, 4], scalar=1.0 / k, in1=art[:, 3],
                                                 op0=ALU.add, op1=ALU.mult).then_inc(art_step, 1)
                    ts(art[:, 5], art[:, 4], 16, 1.0, None, ALU.add)
                    ts(art[:, 10], art[:, 2], 17, SERIES_BELOW, None, ALU.is_lt)
                for p in due_batch(b, t, PRE_BALL + 1, 1):
                    k0 = BALL_STEPS * p
                    ge(dve, ball_step, k0 + 3)
                    dve.reciprocal(ball[:, 3], ball[:, 1]).then_inc(ball_step, 1)
                    ge(dve, ball_step, k0 + 4)
                    dve.scalar_tensor_tensor(out=ball[:, 3], in0=ball[:, 2], scalar=BALL_MAX, in1=ball[:, 3],
                                             op0=ALU.min, op1=ALU.mult).then_inc(ball_step, 1)
                for p, g in due(b, t, PRE_V, 1):
                    ge(dve, ball_step, BALL_STEPS * (p + 1))
                    for c in range(C):
                        last = dve.scalar_tensor_tensor(out=v1[:, g, c], in0=v1[:, g, c], scalar=col(ball[:, 3], g, c),
                                                        in1=x_in[:, g, c], op0=ALU.mult, op1=ALU.add)
                    last.then_inc(v1_done, 1)
                    bn(v1, g, st1, st1_done, v1_done, G * p + g + 1)
                for q, g in due(b, t, POST_H3, -1):
                    ge(dve, x3_ready, G * q + g + 1)
                    ge(dve, agg3_ps, G * q + g - 1)
                    for c in range(C):
                        last = dve.scalar_tensor_tensor(out=h3[:, g % 2, c], in0=res[:, g, c], scalar=col(ln3[:, 10], g, c),
                                                        in1=gamma_row[:, :], op0=ALU.mult, op1=ALU.mult)
                    last.then_inc(h3g_done, 1)
                for q, g in due(b, t, POST_OUT, -1):
                    ge(dve, ln4_step, LN_STEPS * (q + 1))
                    for c in range(C):
                        last = dve.tensor_scalar(v4[:, g, c], v4[:, g, c], col(ln4[:, RSTD], g, c),
                                                 col(ln4[:, SHIFT], g, c), ALU.mult, ALU.add)
                    last.then_inc(out_ready, 1)
                if t == PRE_ART - 1:
                    if live(b - 1):
                        ge(dve, dinv_mid_done, b)
                        ge(dve, v3_done, G * (b - 1))
                        dve.tensor_copy(dinv_post[:, :], dinv_mid[:, :])\
                            .then_inc(dinv_post_done, 1)
                    if live(b):
                        ge(dve, dinv_pre_done, b + 1)
                        ge(dve, dinv_post_done, b)
                        dve.tensor_copy(dinv_mid[:, :], dinv_pre[:, :])\
                            .then_inc(dinv_mid_done, 1)
                for q in due_batch(b, t, POST_LN2, -1):
                    ln_dve(dve, st2, ln2, ln2_step, LN_STEPS, q, st2_done)
                for q in due_batch(b, t, POST_LN4, -1):
                    ln_dve(dve, st4, ln4, ln4_step, LN_STEPS, q, st4_done, EPS / 4)
                for p in due_batch(b, t, PRE_LN, 1):
                    ln_dve(dve, st1, ln1, ln1_step, LN_STEPS, p, st1_done)
                for q in due_batch(b, t, POST_LN3, -1):
                    ln_dve(dve, st3, ln3, ln3_step, LN3_STEPS, q, st3_done)
                    k0 = LN3_STEPS * q
                    ge(dve, ln3_step, k0 + 7)
                    dve.reciprocal(ln3[:, 9], ln3[:, 8]).then_inc(ln3_step, 1)
                    ge(dve, ln3_step, k0 + 8)
                    dve.tensor_tensor(ln3[:, 9], ln3[:, 9], ln3[:, VAR], ALU.mult).then_inc(ln3_step, 1)
                    ge(dve, ln3_step, k0 + 9)
                    dve.tensor_scalar(ln3[:, 9], ln3[:, 9], EPS, None, ALU.add).then_inc(ln3_step, 1)
                for p in due_batch(b, t, PRE_ART, 1):
                    ge(dve, sumsq_done, G * p + G)
                    dve.tensor_scalar(art[:, 0], sumsq[:, :], TINY_SQ, None, ALU.max).then_inc(art_step, 1)
                for p in due_batch(b, t, PRE_BALL, 1):
                    ge(dve, sup_sq_done, G * p + G)
                    dve.tensor_scalar(ball[:, 0], sup_sq[:, :], TINY_SQ, None, ALU.max).then_inc(ball_step, 1)
                for p, g in due(b, t, PRE_IN, 1):
                    if g == 0:
                        ge(dve, dinv_pre_done, p)
                    ge(dve, adj_off_done, G * p + g + 1)
                    dve.tensor_reduce(degree[:, C * g:C * g + C], adj_off[:, g % 2], AX.X, ALU.add)\
                        .then_inc(degree_done, 1)
                if t >= S - G and live(b + 1):
                    g = t - (S - G)
                    ge(dve, agg_ps, S * b + t + 1)
                    ge(dve, adj_loaded[g], 16 * (b + 2))
                    dve.tensor_scalar(linked[:, g], adj_in[:, g].rearrange("p c j -> p (c j)"), 0.0, None,
                                      ALU.not_equal).then_inc(linked_ready, 1)
                for q, g in due(b, t, POST_Y, -1):
                    ge(dve, y_ps, G * q + g + 1)
                    for c in range(C):
                        last = dve.scalar_tensor_tensor(out=res[:, g, c], in0=p_a[:, P * c:P * c + P],
                                                        scalar=col(dinv_post, g, c), in1=res[:, g, c],
                                                        op0=ALU.mult, op1=ALU.add)
                    last.then_inc(v3_done, 1)
                    bn(res, g, st3, st3_done, v3_done, G * q + g + 1)
                for q, g in due(b, t, POST_V2, -1):
                    ge(dve, hT_ps, G * q + g + 1)
                    ge(dve, mask_in, 16 * (q + 1))
                    ge(dve, x1_post_in[g], 16 * (q + 1))
                    for c in range(C):
                        last = dve.scalar_tensor_tensor(out=res[:, g, c], in0=p_b[:, P * c:P * c + P],
                                                        scalar=col(mask_post, g, c), in1=x1_post[:, g, c],
                                                        op0=ALU.mult, op1=ALU.add)
                    last.then_inc(v2_done, 1)
                    bn(res, g, st2, st2_done, v2_done, G * q + g + 1)
            run(dve, slot)

        @block.tensor
        def _(pe):
            def turn(dst, src, n, identity=ident):
                for k in range(n):
                    last = pe.transpose(dst[:, P * k:P * k + P], src(k), identity[:, :])
                return last

            pe.wait_ge(s_const, 8)
            pe.wait_ge(s_w[0], 16)
            turn(p_hn, lambda k: w_ih_n[:, k], 3).then_inc(s_set_pe, 1)
            pe.wait_ge(s_w[1], 16)
            turn(p_r, lambda k: weight_n[:, k], C).then_inc(s_set_pe, 1)
            turn(p_in, lambda k: weight_n[:, C + k], L - C).then_inc(s_set_pe, 1)
            pe.wait_ge(s_w[5], 16)
            turn(p_z, lambda k: mask_n[:, :], 1).then_inc(s_set_pe, 1)
            pe.wait_ge(s_w[6], 16)
            pe.wait_ge(s_set_act, SET_MASK)
            turn(p_z[:, P:2 * P], lambda k: w2_n[:, :], 1).then_inc(s_set_pe, 1)
            pe.wait_ge(s_set_act, SET_W2)
            for k in range(3):
                pe.matmul((p_hn, p_r, p_in)[k][:, :], w_ihT[:, k], weightT[:, 0:W], start=True, stop=True)\
                    .then_inc(s_set_pe, 1)
            for k in range(3):
                last = pe.matmul(p_agg[:, P * k:P * k + P], w_ihT[:, k], weightT[:, W:L * P], start=True, stop=True)
            last.then_inc(s_set_pe, 1)
            pe.wait_ge(s_set_dve, 13)
            for l in range(L + 1):
                if l >= 2:
                    pe.wait_ge(s_set_dve, 15 + l - 1)
                src = (lambda k: vT[:, k, P * l:P * l + P]) if l < L else (lambda k: w_hh_n[:, k])
                turn((p_a, p_b)[l % 2], src, 3).then_inc(s_set_pe, 1)
            pe.wait_ge(s_set_dve, 15 + L + 1)
            for k in range(8, 13):
                pe.wait_ge(s_w[k], 16)
            pe.wait_ge(s_w[7], 16)
            pe.wait_ge(s_half, 3)

            reader = {"a": None, "b": None}

            def claim(b, bank):
                if reader[bank]:
                    s, per, off, c = reader[bank]
                    ge(pe, s, per * (b + off) + c)

            def read_by(b, bank, s, batch_off, g):
                reader[bank] = (s, G, batch_off, g + 1)

            def next_iteration():
                for k, v in reader.items():
                    if v:
                        reader[k] = (v[0], v[1], v[2] - 1, v[3])

            def split3(bank, hi, lo, xh, xl, start, stop, before_lo=None):
                pe.matmul(bank[:, :], hi, xh, start=start, stop=False)
                pe.matmul(bank[:, :], lo, xh, start=False, stop=False)
                if before_lo:
                    before_lo()
                return pe.matmul(bank[:, :], hi, xl, start=False, stop=stop)

            def off_of(first, g, ahead):
                return ahead - (first + g) // S

            def aggregate(b, t):
                g = t % G
                n_old = n_first if t < G else n_st
                if t < G:
                    ge(pe, n_first_lo, G * b + g + 1)
                    ge(pe, linked_ready, G * b + g + 1)
                else:
                    ge(pe, n_ready, SN * b + t - G + 1)
                ge(pe, agg_lo_ready, S * b + t)
                for c in range(C):
                    for part in range(2):
                        last = pe.matmul(p_agg[:, P * c:P * c + P], n_old[:, g, part, c], linked[:, g, P * c:P * c + P],
                                         start=(part == 0), stop=(part == 1))
                last.then_inc(agg_ps, 1)

            def slot(b, t):
                g0, l, n = t % G, t // G, S * b + t
                if live(b):
                    if l == 0:
                        ge(pe, hl_first_ready, G * b + g0 + 1)
                        hh, hl = hh_first[:, g0], hl_first[:, g0]
                    else:
                        ge(pe, hl_ready, SN * b + t - G + 1)
                        hh, hl = hh_st[:, g0], hl_st[:, g0]
                    ah, al = agg_hi[:, t % 2], agg_lo[:, t % 2]
                    ge(pe, t_done, n)
                    split3(p_hn, u_hi[:, 2], u_lo[:, 2], hh, hl, True, True).then_inc(gates_ps, 1)
                    ge(pe, r_ready, n)
                    split3(p_r, u_hi[:, 0], u_lo[:, 0], hh, hl, True, False)
                    ge(pe, agg_hi_ready, n + 1)
                    split3(p_r, v_hi[:, l, 0], v_lo[:, l, 0], ah, al, False, True,
                           lambda: ge(pe, agg_lo_ready, n + 1)).then_inc(gates_ps, 1)
                for p, g in due(b, t, PRE_MM, 1):
                    ge(pe, x_tan_ready, G * p + g + 1)
                    claim(b, "a")
                    for c in range(C):
                        last = pe.matmul(p_a[:, P * c:P * c + P], adjT_pre[:, g, c], x_tan[:, g % 2, c],
                                         start=True, stop=True)
                    last.then_inc(sup_ps, 1)
                    read_by(b, "a", sup_ready, off_of(PRE_MM, g, 1), g)
                for p, g in due(b, t, PRE_X1T, 1):
                    ge(pe, x1_ready, G * p + g + 1)
                    claim(b, "a")
                    turn(p_a, lambda c: x1_pre[:, g, c], C).then_inc(x1T_ps, 1)
                    read_by(b, "a", hh_first_ready, off_of(PRE_X1T, g, 1), g)
                for q, g in due(b, t, POST_CONV, -1):
                    ge(pe, h3T_ready, G * q + g + 1)
                    ge(pe, agg3_ready, G * q + min(g + 2, G))
                    claim(b, "b")
                    for c in range(C):
                        o = p_b[:, P * c:P * c + P]
                        pe.matmul(o, agg3[:, g % 2, P * c:P * c + P], w_rel_s[:, :], start=True, stop=False)
                        last = pe.matmul(o, h3T[:, g % 2, P * c:P * c + P], w_root_s[:, :], start=False, stop=True)
                    last.then_inc(conv_ps, 1)
                    read_by(b, "b", conv_done, off_of(POST_CONV, g, -1), g)
                for q, g in due(b, t, POST_X2T, -1):
                    ge(pe, x2_ready, G * q + g + 1)
                    claim(b, "b")
                    turn(p_b, lambda c: res[:, g, c], C).then_inc(x2T_ps, 1)
                    read_by(b, "b", x2T_ready, off_of(POST_X2T, g, -1), g)
                for m, u in following(b, t):
                    aggregate(m, u)
                if live(b):
                    ge(pe, t2_done, n)
                    split3(p_in, v_hi[:, l, 2], v_lo[:, l, 2], ah, al, True, True).then_inc(gates_ps, 1)
                    ge(pe, z_ready, n)
                    split3(p_z, u_hi[:, 1], u_lo[:, 1], hh, hl, True, False)
                    split3(p_z, v_hi[:, l, 1], v_lo[:, l, 1], ah, al, False, True).then_inc(gates_ps, 1)
                if live(b) and 2 <= t < SN + 2:
                    u = t - 2
                    ge(pe, hl_ready, SN * b + u + 1)
                    ge(pe, n_ready, SN * b + u)
                    turn(p_nt, lambda c: hh_st[:, u % G, P * c:P * c + P], C, ident16)
                    turn(p_nt[:, W:2 * W], lambda c: hl_st[:, u % G, P * c:P * c + P], C, ident16).then_inc(nt_ps, 1)
                for p, g in due(b, t, PRE_IN, 1):
                    ge(pe, adj_loaded[g], 16 * (p + 1))
                    claim(b, "a")
                    turn(p_a, lambda c: adj_in[:, g, c], C).then_inc(adjT_ps, 1)
                    read_by(b, "a", adjT_ready, off_of(PRE_IN, g, 1), g)
                for q, g in due(b, t, POST_V2, -1):
                    ge(pe, h_done, S * q + S - G + g + 1)
                    claim(b, "b")
                    turn(p_b, lambda c: h_st[:, g, P * c:P * c + P], C).then_inc(hT_ps, 1)
                    read_by(b, "b", v2_done, off_of(POST_V2, g, -1), g)
                for q, g in due(b, t, POST_H, -1):
                    ge(pe, x2T_ready, G * q + g + 1)
                    claim(b, "b")
                    for c in range(C):
                        last = pe.matmul(p_b[:, P * c:P * c + P], x2T[:, g % 2, P * c:P * c + P], w2T[:, :],
                                         start=True, stop=True)
                    last.then_inc(h2_ps, 1)
                    read_by(b, "b", h2b_done, off_of(POST_H, g, -1), g)
                for q, g in due(b, t, POST_Y, -1):
                    ge(pe, h2s_ready, G * q + g + 1)
                    ge(pe, adjT_post_in[g], 16 * (q + 1))
                    claim(b, "a")
                    for c in range(C):
                        last = pe.matmul(p_a[:, P * c:P * c + P], adjT_post[:, g, c], h2[:, g % 2, c],
                                         start=True, stop=True)
                    last.then_inc(y_ps, 1)
                    read_by(b, "a", v3_done, off_of(POST_Y, g, -1), g)
                for q, g in due(b, t, POST_AGG, -1):
                    ge(pe, h3_ready, G * q + g + 1)
                    claim(b, "a")
                    turn(p_a, lambda c: h3[:, g % 2, c], C).then_inc(h3T_ps, 1)
                    read_by(b, "a", h3T_ready, off_of(POST_AGG, g, -1), g)
                    claim(b, "b")
                    for c in range(C):
                        last = pe.matmul(p_b[:, P * c:P * c + P], h3[:, g % 2, c], adjT_post[:, g, c],
                                         start=True, stop=True)
                    last.then_inc(agg3_ps, 1)
                    read_by(b, "b", agg3_ready, off_of(POST_AGG, g, -1), g)
                if t == S - 1:
                    next_iteration()
            run(pe, slot)


_INS = ['x', 'adj', 'nodemask', 'L1_gnn_weight', 'L1_gnn_w_ih', 'L1_gnn_w_hh', 'L1_gnn_b_ih', 'L1_gnn_b_hh',
        'L2_gnn_W', 'L2_gnn_b', 'L3_gnn_W_rel', 'L3_gnn_b_rel', 'L3_gnn_W_root', 'L3_gnn_ln_gamma', 'L3_gnn_ln_beta']
_OUTS = [((128, 128, 128), 'float32')]


def kernel(**inputs):
    import numpy as _np
    import concourse.bacc as _bacc
    from concourse import mybir as _mybir
    from concourse.bass_utils import run_bass_kernel_spmd as _run

    nc = _bacc.Bacc("TRN2", target_bir_lowering=False, num_devices=1)
    arrays, args = {}, []
    for name in _INS:
        a = _np.ascontiguousarray(inputs[name])
        arrays[f"in_{name}_dram"] = a
        args.append(nc.dram_tensor(f"in_{name}_dram", a.shape, _mybir.dt.from_np(a.dtype), kind="ExternalInput").ap())
    for i, (shape, dtype) in enumerate(_OUTS):
        dt = _mybir.dt.from_np(_np.dtype(dtype))
        args.append(nc.dram_tensor(f"out_{i}_dram", shape, dt, kind="ExternalOutput").ap())
    build(nc, *args)
    r = _run(nc, [arrays], core_ids=[0])
    got = tuple(r.results[0][f"out_{i}_dram"] for i in range(len(_OUTS)))
    return got[0]
```

```python
from contextlib import ExitStack

import concourse.bass as bass
from concourse import mybir

F32 = mybir.dt.float32
F16 = mybir.dt.float16
I32 = mybir.dt.int32
ALU = mybir.AluOpType
ACT = mybir.ActivationFunctionType
AX = mybir.AxisListType

P = 128
C = 4
G = 4
W = C * P
BG = G * C

EPS = 1e-5
TINY_SQ = 1e-30
ATANH_MAX = 1.0 - 1e-7
BALL_MAX = 1.0 - 0.004
SERIES_BELOW = 0.25
SERIES = (11, 9, 7, 5, 3)
SCALE_EXP = 8

PRE_IN, PRE_ART, PRE_XT, PRE_MM, PRE_BALL, PRE_V, PRE_LN, PRE_X1, PRE_X1T = 0, 4, 6, 7, 11, 12, 15, 16, 18
PRE_DINV = 11
POST_V2, POST_LN2, POST_X2, POST_X2T, POST_H, POST_Y = 0, 4, 5, 6, 6, 8
POST_LN3, POST_X3, POST_H3, POST_AGG, POST_CONV, POST_LN4, POST_OUT = 12, 13, 14, 15, 17, 21, 23

ART_STEPS = 18
BALL_STEPS = 2
LN_STEPS = 7
LN3_STEPS = 11


def build(nc, x, adj, nodemask, weight, w_ih, w_hh, b_ih, b_hh, w2, b2, w_rel, b_rel, w_root, gamma, beta, out):
    NB = x.shape[0] // BG
    L = weight.shape[0]
    S = L * G
    SN = S - G
    LOOP0, LOOP1 = 2, NB - 2

    with ExitStack() as ctx:
        def sb(name, shape, dt=F32):
            return ctx.enter_context(nc.sbuf_tensor(name, shape, dt))

        def pb(name, dt=F32):
            return ctx.enter_context(nc.psum_tensor(name, [P, 2048 // mybir.dt.size(dt)], dt))

        def sem(name):
            return ctx.enter_context(nc.semaphore(name))

        def sems(name, n):
            return [sem(f"{name}{i}") for i in range(n)]

        ident = sb("ident", [P, P])
        ident16 = sb("ident16", [P, P], F16)
        offdiag = sb("offdiag", [P, P])
        half16 = sb("half16", [P, 2, BG])
        w_hh_n = sb("w_hh_n", [P, 3, P])
        v_hi = sb("v_hi", [P, L, 3, P], F16)
        v_lo = sb("v_lo", [P, L, 3, P], F16)
        u_hi = sb("u_hi", [P, 3, P], F16)
        u_lo = sb("u_lo", [P, 3, P], F16)
        rowmax = sb("rowmax", [P, 3, 3])
        up = sb("up", [P, 3])
        down = sb("down", [P, 3])
        bi = sb("bi", [P, 3])
        bh = sb("bh", [P, 3])
        bias_rz = sb("bias_rz", [P, 3])
        bias_hn = sb("bias_hn", [P, 1])
        w2_n = sb("w2_n", [P, P])
        w2T = sb("w2T", [P, P])
        b2_row = sb("b2_row", [P, P])
        w_rel_s = sb("w_rel_s", [P, P])
        w_root_s = sb("w_root_s", [P, P])
        b_rel_row = sb("b_rel_row", [P, P])
        gamma_row = sb("gamma_row", [P, P])
        beta_row = sb("beta_row", [P, P])
        mask_n = sb("mask_n", [P, P])
        maskT = sb("maskT", [P, P])

        x_in = sb("x_in", [P, G, C, P])
        adj_in = sb("adj_in", [P, G, C, P])
        adj_off = sb("adj_off", [P, 2, C, P])
        adjT_pre = sb("adjT_pre", [P, G, C, P])
        x_tan = sb("x_tan", [P, 2, C, P])
        v1 = sb("v1", [P, G, C, P])
        x1_pre = sb("x1_pre", [P, G, C, P])
        act_junk = sb("act_junk", [P, C, P], F16)
        sumsq = sb("sumsq", [P, BG])
        art = sb("art", [P, 12, BG])
        tan_scale = sb("tan_scale", [P, BG])
        sup_sq = sb("sup_sq", [P, BG])
        ball = sb("ball", [P, 4, BG])
        degree = sb("degree", [P, BG])
        dinv_pre = sb("dinv_pre", [P, BG])
        dinv_mid = sb("dinv_mid", [P, BG])
        dinv_post = sb("dinv_post", [P, BG])
        st1, st2, st3, st4 = (sb(f"st{i}", [P, BG, 6]) for i in range(1, 5))
        ln1, ln2, ln4 = (sb(f"ln{i}", [P, 9, BG]) for i in (1, 2, 4))
        ln3 = sb("ln3", [P, 11, BG])

        linked = sb("linked", [P, G, W], F16)
        n_first = sb("n_first", [P, G, 2, C, P], F16)
        h_first = sb("h_first", [P, G, W])
        hh_first = sb("hh_first", [P, G, W], F16)
        hl_first = sb("hl_first", [P, G, W], F16)
        n_st = sb("n_st", [P, G, 2, C, P], F16)
        h_st = sb("h_st", [P, G, W])
        hh_st = sb("hh_st", [P, G, W], F16)
        hl_st = sb("hl_st", [P, G, W], F16)
        agg_hi = sb("agg_hi", [P, 2, W], F16)
        agg_lo = sb("agg_lo", [P, 2, W], F16)
        r_s = sb("r_s", [P, 2, W])
        z_s = sb("z_s", [P, 2, W])
        t_s = sb("t_s", [P, 2, W])
        c_s = sb("c_s", [P, 2, W])
        d_s = sb("d_s", [P, 2, W])

        adjT_mid = sb("adjT_mid", [P, G, C, P])
        adjT_post = sb("adjT_post", [P, G, C, P])
        x1_post = sb("x1_post", [P, G, C, P])
        mask_post = sb("mask_post", [P, BG])
        res = sb("res", [P, G, C, P])
        x2T = sb("x2T", [P, 2, W])
        h2 = sb("h2", [P, 2, C, P])
        h3 = sb("h3", [P, 2, C, P])
        h3T = sb("h3T", [P, 2, W])
        agg3 = sb("agg3", [P, 2, W])
        v4 = sb("v4", [P, G, C, P])

        res_flat = res[:, :, :, :].rearrange("p g c d -> p (g c d)")
        w_ih_n = res_flat[:, 0:3 * P].rearrange("p (k c) -> p k c", k=3)
        w_ihT = res_flat[:, 3 * P:6 * P].rearrange("p (k c) -> p k c", k=3)
        weight_n = res_flat[:, 6 * P:(6 + L) * P].rearrange("p (l c) -> p l c", l=L)
        weightT = res_flat[:, (6 + L) * P:(6 + 2 * L) * P]
        vT = v4[:, :, :, :].rearrange("p g c d -> p (g c d)")[:, 0:3 * L * P].rearrange("p (k c) -> p k c", k=3)

        p_hn, p_r, p_in, p_z, p_agg = (pb(f"p_{n}") for n in ("hn", "r", "in", "z", "agg"))
        p_nt = pb("p_nt", F16)
        p_a, p_b = pb("p_a"), pb("p_b")
        banks = {"a": p_a, "b": p_b}

        s_w = sems("s_w", 14)
        s_const = sem("s_const")
        s_set_pe = sem("s_set_pe")
        s_set_dve = sem("s_set_dve")
        s_half = sem("s_half")
        s_set_act = sem("s_set_act")
        x_loaded, adj_loaded = sems("x_loaded", G), sems("adj_loaded", G)
        adjT_mid_in, adjT_post_in, x1_post_in = sems("adjT_mid_in", G), sems("adjT_post_in", G), sems("x1_post_in", G)
        mask_in = sem("mask_in")
        out_stored = sems("out_stored", G)
        names = """sumsq_done adj_off_done degree_done adjT_ps adjT_ready art_step art_ln_done dinv_pre_done dinv_mid_done
            dinv_post_done x_tan_ready sup_ps sup_ready sup_sq_done ball_step v1_done st1_done ln1_step x1_ready
            n_first_hi n_first_lo x1T_ps h_first_ready hh_first_ready hl_first_ready linked_ready
            agg_ps agg_hi_ready agg_lo_ready gates_ps r_ready t_done t2_done cand_ready z_ready d_ready zd_done h_done
            hh_ready hl_ready nt_ps n_ready
            hT_ps v2_done st2_done ln2_step x2_ready x2T_ps x2T_ready h2_ps h2b_done h2s_ready y_ps v3_done st3_done
            ln3_step x3_ready h3g_done h3_ready h3T_ps agg3_ps h3T_ready agg3_ready conv_ps conv_done v4_done
            st4_done ln4_step out_ready
            art_norm art_max ball_max ball_norm ball_tanh ln1_pow ln2_pow ln3_pow ln4_pow ln1_ready ln2_ready ln3_ready ln3_factor ln4_ready""".split()
        (sumsq_done, adj_off_done, degree_done, adjT_ps, adjT_ready, art_step, art_ln_done, dinv_pre_done, dinv_mid_done,
         dinv_post_done, x_tan_ready, sup_ps, sup_ready, sup_sq_done, ball_step, v1_done, st1_done, ln1_step, x1_ready,
         n_first_hi, n_first_lo, x1T_ps, h_first_ready, hh_first_ready, hl_first_ready, linked_ready,
         agg_ps, agg_hi_ready, agg_lo_ready, gates_ps, r_ready, t_done, t2_done, cand_ready, z_ready, d_ready,
         zd_done, h_done, hh_ready, hl_ready, nt_ps, n_ready,
         hT_ps, v2_done, st2_done, ln2_step, x2_ready, x2T_ps, x2T_ready, h2_ps, h2b_done, h2s_ready, y_ps, v3_done,
         st3_done, ln3_step, x3_ready, h3g_done, h3_ready, h3T_ps, agg3_ps, h3T_ready, agg3_ready, conv_ps, conv_done,
         v4_done, st4_done, ln4_step, out_ready,
         art_norm, art_max, ball_max, ball_norm, ball_tanh, ln1_pow, ln2_pow, ln3_pow, ln4_pow, ln1_ready, ln2_ready, ln3_ready, ln3_factor, ln4_ready) = (sem(n) for n in names)

        def ge(eng, s, value):
            if not isinstance(value, int) or value > 0:
                eng.wait_ge(s, value)

        def live(batch):
            return not isinstance(batch, int) or 0 <= batch < NB

        def due(b, t, first, ahead):
            for g in range(G):
                if (first + g) % S == t:
                    batch = b + ahead - (first + g) // S
                    if live(batch):
                        yield batch, g

        def due_batch(b, t, first, ahead):
            batch = b + ahead - first // S
            return [batch] if first % S == t and live(batch) else []

        def earlier(b, t, back):
            batch, slot = (b, t - back) if t >= back else (b - 1, t - back + S)
            return [(batch, slot)] if live(batch) else []

        def following(b, t):
            batch, slot = (b, t + 1) if t < S - 1 else (b + 1, 0)
            return [(batch, slot)] if live(batch) else []

        def run(eng, slot):
            for b in range(-1, LOOP0):
                for t in range(S):
                    slot(b, t)
            with eng.Fori(LOOP0, LOOP1) as b:
                for t in range(S):
                    slot(b, t)
            for b in range(LOOP1, NB + 2):
                for t in range(S):
                    slot(b, t)

        def graphs(row):
            return row[:, :].unsqueeze(1).broadcast_to([P, C, P])

        def columns(small, g):
            return small[:, C * g:C * g + C].unsqueeze(2).broadcast_to([P, C, P])

        def col(small, g, c):
            return small[:, C * g + c:C * g + c + 1]

        NEG_MEAN, VAR, RSTD, SHIFT, VAR_EPS = 0, 5, 6, 7, 8

        def ln_dve(dve, st, ln, step, steps, batch, st_done, eps=EPS):
            me, mo, qe, qo = st[:, :, 1], st[:, :, 4], st[:, :, 2], st[:, :, 5]
            ge(dve, st_done, G * batch + G)
            dve.tensor_tensor(ln[:, 1], me, mo, ALU.subtract).then_inc(step, 1)
            dve.tensor_tensor(ln[:, 0], me, mo, ALU.add).then_inc(step, 1)
            dve.tensor_tensor(ln[:, 2], qe, qo, ALU.add).then_inc(step, 1)
            ge(dve, step, steps * batch + 1)
            dve.tensor_tensor(ln[:, 3], ln[:, 1], ln[:, 1], ALU.mult).then_inc(step, 1)
            ge(dve, step, steps * batch + 2)
            dve.tensor_scalar(ln[:, NEG_MEAN], ln[:, 0], -0.5, None, ALU.mult).then_inc(step, 1)
            ge(dve, step, steps * batch + 4)
            dve.scalar_tensor_tensor(out=ln[:, 4], in0=ln[:, 3], scalar=P / 4.0, in1=ln[:, 2],
                                     op0=ALU.mult, op1=ALU.add).then_inc(step, 1)
            ge(dve, step, steps * batch + 6)
            dve.tensor_scalar(ln[:, VAR_EPS], ln[:, 4], 1.0 / P, eps, ALU.mult, ALU.add).then_inc(step, 1)

        def ln_pool(pool, ln, step, steps, batch, g, powered, done):
            part = slice(C * g, C * g + C)
            ge(pool, step, steps * (batch + 1))
            pool.tensor_tensor(ln[:, RSTD, part], ln[:, VAR_EPS, part], half16[:, 1, part], ALU.pow).then_inc(powered, 1)
            ge(pool, powered, G * batch + g + 1)
            pool.tensor_tensor(ln[:, SHIFT, part], ln[:, NEG_MEAN, part], ln[:, RSTD, part], ALU.mult).then_inc(done, 1)

        SET_MASK, SET_W2, SET_V = 4, 5, 9

        block = ctx.enter_context(nc.Block())

        @block.sync
        def _(sp):
            def load_x(at, g):
                src = x[bass.ds(at, C), :, :].rearrange("c n d -> n c d")
                sp.dma_start(x_in[:, g], src).then_inc(x_loaded[g], 16)

            def load_adj(at, g):
                src = adj[bass.ds(at, C), :, :].rearrange("c i j -> i c j")
                sp.dma_start(adj_in[:, g], src).then_inc(adj_loaded[g], 16)

            for g in range(G):
                load_x(C * g, g)
                load_adj(C * g, g)
            loads = [
                (w_ih_n[:, :, :], w_ih.rearrange("(k p) c -> p k c", p=P)),
                (weight_n[:, :, :], weight.rearrange("l d c -> d l c")),
                (w_hh_n[:, :, :], w_hh.rearrange("(k p) c -> p k c", p=P)),
                (bi[:, :], b_ih.rearrange("(k p) -> p k", p=P)),
                (bh[:, :], b_hh.rearrange("(k p) -> p k", p=P)),
                (mask_n[:, :], nodemask),
                (w2_n[:, :], w2),
                (b2_row[:, :], b2.partition_broadcast(P)),
                (w_rel_s[:, :], w_rel),
                (w_root_s[:, :], w_root),
                (b_rel_row[:, :], b_rel.partition_broadcast(P)),
                (gamma_row[:, :], gamma.partition_broadcast(P)),
                (beta_row[:, :], beta.partition_broadcast(P)),
            ]
            for (dst, src), s in zip(loads, s_w):
                sp.dma_start(dst, src, allow_slow_non_contiguous=True).then_inc(s, 16)

            def counts(*values):
                return [v if isinstance(v, int) else sp.compute_val(v) for v in values]

            def slot(b, t):
                for q, g in due(b, t, POST_OUT, -1):
                    at, rows = counts(q * BG + C * g, G * q + g + 1)
                    ge(sp, out_ready, rows)
                    dst = out[bass.ds(at, C), :, :].rearrange("c n d -> n c d")
                    sp.dma_start(dst, v4[:, g]).then_inc(out_stored[g], 16)
                if t == 5 and live(b):
                    at, read = counts(b * BG, G * b)
                    ge(sp, s_set_act, SET_MASK)
                    ge(sp, v2_done, read)
                    sp.dma_start(mask_post[:, :], maskT[:, bass.ds(at, BG)]).then_inc(mask_in, 16)
                    for g in range(G):
                        x1_there, = counts(G * b + g + 1)
                        ge(sp, x1_ready, x1_there)
                        sp.dma_start(x1_post[:, g], x1_pre[:, g]).then_inc(x1_post_in[g], 16)
                if t >= S - G - 1 and t < S - 1 and live(b + 2):
                    g = t - (S - G - 1)
                    at, read = counts((b + 2) * BG + C * g, G * (b + 1) + g + 1)
                    ge(sp, v1_done, read)
                    load_x(at, g)
                if t >= S - G:
                    g = t - (S - G)
                    if live(b + 2):
                        at, read = counts((b + 2) * BG + C * g, G * (b + 1) + g + 1)
                        ge(sp, linked_ready, read)
                        load_adj(at, g)
                    if live(b):
                        read, there = counts(G * (b - 1) + g + 1, 16 * (b + 1))
                        ge(sp, agg3_ps, read)
                        ge(sp, adjT_mid_in[g], there)
                        sp.dma_start(adjT_post[:, g], adjT_mid[:, g]).then_inc(adjT_post_in[g], 16)
                    if live(b + 1):
                        moved, there = counts(16 * (b + 1), G * (b + 1) + g + 1)
                        ge(sp, adjT_post_in[g], moved)
                        ge(sp, adjT_ready, there)
                        sp.dma_start(adjT_mid[:, g], adjT_pre[:, g]).then_inc(adjT_mid_in[g], 16)
            run(sp, slot)
            for g in range(G):
                sp.wait_ge(out_stored[g], 16 * NB)

        @block.gpsimd
        def _(pool):
            pool.memset(ident[:, :], 0.0).then_inc(s_const, 1)
            pool.memset(ident16[:, :], 0.0).then_inc(s_const, 1)
            pool.memset(offdiag[:, :], 1.0).then_inc(s_const, 1)
            pool.memset(half16[:, 0], 0.5).then_inc(s_const, 1)
            pool.memset(half16[:, 1], -0.5).then_inc(s_const, 1)
            pool.wait_ge(s_const, 5)
            for tile, fill in ((ident, 1.0), (ident16, 1.0), (offdiag, 0.0)):
                pool.affine_select(out=tile[:, :], in_=tile[:, :], compare_op=ALU.not_equal, fill=fill, base=0,
                                   pattern=[[-1, P]], channel_multiplier=1).then_inc(s_const, 1)
            pool.wait_ge(s_const, 8)

            def slot(b, t):
                for m, u in earlier(b, t, 2):
                    if u < SN:
                        ge(pool, hh_ready, SN * m + u + 1)
                        pool.tensor_tensor(hl_st[:, u % G], h_st[:, u % G], hh_st[:, u % G], ALU.subtract)\
                            .then_inc(hl_ready, 1)
                for m, u in earlier(b, t, 1):
                    h_old = h_first if u < G else h_st
                    ge(pool, cand_ready, S * m + u + 1)
                    pool.tensor_tensor(d_s[:, u % 2], h_old[:, u % G], c_s[:, u % 2], ALU.subtract).then_inc(d_ready, 1)
                for q, g in due(b, t, POST_H + 1, -1):
                    ge(pool, dinv_post_done, q + 1)
                    ge(pool, h2b_done, G * q + g + 1)
                    pool.tensor_tensor(h2[:, g % 2], h2[:, g % 2], columns(dinv_post, g), ALU.mult)\
                        .then_inc(h2s_ready, 1)
                for q, g in due(b, t, POST_H3 + 1, -1):
                    ge(pool, h3g_done, G * q + g + 1)
                    pool.tensor_tensor(h3[:, g % 2], h3[:, g % 2], graphs(beta_row), ALU.add).then_inc(h3_ready, 1)
                for first, ahead, ln, step, steps, powered, ready in (
                        (PRE_LN, 1, ln1, ln1_step, LN_STEPS, ln1_pow, ln1_ready),
                        (POST_LN2, -1, ln2, ln2_step, LN_STEPS, ln2_pow, ln2_ready),
                        (POST_LN3, -1, ln3, ln3_step, LN3_STEPS, ln3_pow, ln3_ready),
                        (POST_LN4, -1, ln4, ln4_step, LN_STEPS, ln4_pow, ln4_ready)):
                    for m, g in due(b, t, first + 1, ahead):
                        ln_pool(pool, ln, step, steps, m, g, powered, ready)
                for q, g in due(b, t, POST_LN3 + 1, -1):
                    part = slice(C * g, C * g + C)
                    pool.tensor_tensor(ln3[:, 10, part], ln3[:, 9, part], half16[:, 1, part], ALU.pow)\
                        .then_inc(ln3_factor, 1)
                for p, g in due(b, t, PRE_IN + 1, 1):
                    part = slice(C * g, C * g + C)
                    ge(pool, art_max, G * p + g + 1)
                    pool.tensor_tensor(art[:, 1, part], art[:, 0, part], half16[:, 0, part], ALU.pow).then_inc(art_norm, 1)
                for p, g in due(b, t, PRE_MM + 1, 1):
                    part = slice(C * g, C * g + C)
                    ge(pool, ball_max, G * p + g + 1)
                    pool.tensor_tensor(ball[:, 1, part], ball[:, 0, part], half16[:, 0, part], ALU.pow)\
                        .then_inc(ball_norm, 1)
                for p, g in due(b, t, PRE_DINV, 1):
                    part = slice(C * g, C * g + C)
                    ge(pool, degree_done, G * p + g + 1)
                    ge(pool, dinv_mid_done, p)
                    pool.tensor_tensor(dinv_pre[:, part], degree[:, part], half16[:, 1, part], ALU.pow)\
                        .then_inc(dinv_pre_done, 1)
                for p, g in due(b, t, PRE_X1 + 1, 1):
                    ge(pool, n_first_hi, G * p + g + 1)
                    pool.tensor_tensor(n_first[:, g, 1], x1_pre[:, g], n_first[:, g, 0], ALU.subtract)\
                        .then_inc(n_first_lo, 1)
                for p, g in due(b, t, PRE_IN, 1):
                    ge(pool, adj_loaded[g], 16 * (p + 1))
                    ge(pool, degree_done, G * p + g - 1)
                    pool.tensor_tensor(adj_off[:, g % 2], adj_in[:, g], graphs(offdiag), ALU.mult)\
                        .then_inc(adj_off_done, 1)
                for p, g in due(b, t, PRE_XT, 1):
                    ge(pool, art_step, ART_STEPS * (p + 1))
                    ge(pool, sup_ps, G * p + g - 1)
                    pool.tensor_tensor(x_tan[:, g % 2], x_in[:, g], columns(tan_scale, g), ALU.mult)\
                        .then_inc(x_tan_ready, 1)
                for p, g in due(b, t, PRE_X1T, 1):
                    ge(pool, hh_first_ready, G * p + g + 1)
                    pool.tensor_tensor(hl_first[:, g], h_first[:, g], hh_first[:, g], ALU.subtract)\
                        .then_inc(hl_first_ready, 1)
            run(pool, slot)

        @block.scalar
        def _(act):
            act.wait_ge(s_set_pe, 1)
            act.activation(w_ihT[:, :, :].rearrange("p k c -> p (k c)"), p_hn[:, 0:3 * P], ACT.Copy).then_inc(s_set_act, 1)
            act.wait_ge(s_set_pe, 2)
            act.activation(weightT[:, 0:W], p_r[:, :], ACT.Copy).then_inc(s_set_act, 1)
            act.wait_ge(s_set_pe, 3)
            act.activation(weightT[:, W:L * P], p_in[:, 0:L * P - W], ACT.Copy).then_inc(s_set_act, 1)
            act.wait_ge(s_set_pe, 4)
            act.activation(maskT[:, :], p_z[:, 0:P], ACT.Copy).then_inc(s_set_act, 1)
            act.wait_ge(s_set_pe, 5)
            act.activation(w2T[:, :], p_z[:, P:2 * P], ACT.Copy).then_inc(s_set_act, 1)
            for k in range(3):
                act.wait_ge(s_set_pe, 6 + k)
                act.activation(vT[:, k, 0:W], (p_hn, p_r, p_in)[k][:, :], ACT.Copy).then_inc(s_set_act, 1)
            act.wait_ge(s_set_pe, 9)
            act.activation(vT[:, :, W:L * P], p_agg[:, 0:3 * P].rearrange("p (k c) -> p k c", k=3), ACT.Copy)\
                .then_inc(s_set_act, 1)
            for l in range(L + 1):
                act.wait_ge(s_set_pe, 10 + l)
                hi = v_hi[:, l] if l < L else u_hi[:, :, :]
                act.activation(hi, (p_a, p_b)[l % 2][:, 0:3 * P].rearrange("p (k c) -> p k c", k=3), ACT.Copy)\
                    .then_inc(s_set_act, 1)

            def apply(dst, src, ln, g, done):
                for c in range(C):
                    last = act.activation(dst[:, g, c], src[:, g, c], ACT.Identity, bias=col(ln[:, SHIFT], g, c),
                                          scale=col(ln[:, RSTD], g, c))
                last.then_inc(done, 1)

            def slot(b, t):
                if live(b):
                    ge(act, gates_ps, 4 * (S * b + t) + 2)
                    act.activation(r_s[:, t % 2], p_r[:, :], ACT.Sigmoid, bias=bias_rz[:, 0:1], scale=down[:, 0:1])\
                        .then_inc(r_ready, 1)
                for m, u in following(b, t):
                    ge(act, agg_ps, S * m + u + 1)
                    act.activation(agg_hi[:, u % 2], p_agg[:, :], ACT.Copy).then_inc(agg_hi_ready, 1)
                for p, g in due(b, t, PRE_X1T, 1):
                    ge(act, x1T_ps, G * p + g + 1)
                    act.activation(h_first[:, g], p_a[:, :], ACT.Copy).then_inc(h_first_ready, 1)
                    act.activation(hh_first[:, g], p_a[:, :], ACT.Copy).then_inc(hh_first_ready, 1)
                for p, g in due(b, t, PRE_MM, 1):
                    ge(act, sup_ps, G * p + g + 1)
                    act.activation(v1[:, g], p_a[:, :].rearrange("p (c d) -> p c d", c=C), ACT.Copy)\
                        .then_inc(sup_ready, 1)
                for q, g in due(b, t, POST_X2T, -1):
                    ge(act, x2T_ps, G * q + g + 1)
                    ge(act, h2_ps, G * q + g - 1)
                    act.activation(x2T[:, g % 2], p_b[:, :], ACT.Copy).then_inc(x2T_ready, 1)
                if live(b):
                    ge(act, gates_ps, 4 * (S * b + t) + 4)
                    ge(act, zd_done, S * b + t - 1)
                    act.activation(z_s[:, t % 2], p_z[:, :], ACT.Sigmoid, bias=bias_rz[:, 1:2], scale=down[:, 1:2])\
                        .then_inc(z_ready, 1)
                    ge(act, t2_done, S * b + t + 1)
                    ge(act, h_done, S * b + t - 1)
                    act.activation(c_s[:, t % 2], t_s[:, t % 2], ACT.Tanh, bias=bi[:, 2:3], scale=down[:, 2:3])\
                        .then_inc(cand_ready, 1)
                for p, g in due(b, t, PRE_X1, 1):
                    ge(act, ln1_ready, G * p + g + 1)
                    ge(act, x1_post_in[g], 16 * p)
                    apply(x1_pre, v1, ln1, g, x1_ready)
                    ge(act, x1_ready, G * p + g + 1)
                    act.activation(n_first[:, g, 0], x1_pre[:, g], ACT.Copy).then_inc(n_first_hi, 1)
                for p, g in due(b, t, PRE_IN, 1):
                    ge(act, adjT_ps, G * p + g + 1)
                    ge(act, adjT_mid_in[g], 16 * p)
                    act.activation(adjT_pre[:, g].rearrange("p c i -> p (c i)"), p_a[:, :], ACT.Copy)\
                        .then_inc(adjT_ready, 1)
                for q, g in due(b, t, POST_AGG, -1):
                    ge(act, h3T_ps, G * q + g + 1)
                    ge(act, conv_ps, G * q + g - 1)
                    act.activation(h3T[:, g % 2], p_a[:, :], ACT.Copy).then_inc(h3T_ready, 1)
                    ge(act, agg3_ps, G * q + g + 1)
                    act.activation(agg3[:, g % 2], p_b[:, :], ACT.Copy).then_inc(agg3_ready, 1)
                for m, u in earlier(b, t, 1):
                    if u < SN:
                        ge(act, h_done, S * m + u + 1)
                        act.activation(hh_st[:, u % G], h_st[:, u % G], ACT.Copy).then_inc(hh_ready, 1)
                for q, g in due(b, t, POST_X2, -1):
                    ge(act, ln2_ready, G * q + g + 1)
                    apply(res, res, ln2, g, x2_ready)
                for q, g in due(b, t, POST_X3, -1):
                    ge(act, ln3_ready, G * q + g + 1)
                    apply(res, res, ln3, g, x3_ready)
                for p in due_batch(b, t, PRE_ART + 1, 1):
                    ge(act, art_step, ART_STEPS * p + 7)
                    act.activation(art[:, 11], art[:, 7], ACT.Ln).then_inc(art_ln_done, 1)
                for p in due_batch(b, t, PRE_BALL, 1):
                    ge(act, ball_norm, G * (p + 1))
                    act.activation(ball[:, 2], ball[:, 1], ACT.Tanh).then_inc(ball_tanh, 1)
                for p, g in due(b, t, PRE_IN, 1):
                    ge(act, x_loaded[g], 16 * (p + 1))
                    ge(act, sumsq_done, G * p + g)
                    for c in range(C):
                        last = act.activation(act_junk[:, c], x_in[:, g, c], ACT.Square, accum_out=col(sumsq, g, c))
                    last.then_inc(sumsq_done, 1)
                for p, g in due(b, t, PRE_MM, 1):
                    ge(act, sup_ready, G * p + g + 1)
                    ge(act, sup_sq_done, G * p + g)
                    for c in range(C):
                        last = act.activation(act_junk[:, c], v1[:, g, c], ACT.Square, accum_out=col(sup_sq, g, c))
                    last.then_inc(sup_sq_done, 1)
            run(act, slot)

        @block.vector
        def _(dve):
            dve.wait_ge(s_w[2], 16)
            dve.tensor_reduce(rowmax[:, :, 0], w_hh_n[:, :, :], AX.X, ALU.max, apply_absolute_value=True)\
                .then_inc(s_set_dve, 1)
            dve.wait_ge(s_set_act, SET_V)
            dve.tensor_reduce(rowmax[:, :, 1], vT[:, :, :], AX.X, ALU.max, apply_absolute_value=True)\
                .then_inc(s_set_dve, 1)
            dve.wait_ge(s_set_dve, 2)
            dve.tensor_tensor(rowmax[:, :, 2], rowmax[:, :, 0], rowmax[:, :, 1], ALU.max).then_inc(s_set_dve, 1)
            dve.wait_ge(s_set_dve, 3)
            dve.tensor_scalar(up[:, :], rowmax[:, :, 2], 2.0 ** -100, 2.0 ** 100, ALU.max, ALU.min).then_inc(s_set_dve, 1)
            dve.wait_ge(s_set_dve, 4)
            down_i, up_i = down[:, :].bitcast(I32), up[:, :].bitcast(I32)
            dve.tensor_scalar(down_i, up_i, 0x7F800000, None, ALU.bitwise_and).then_inc(s_set_dve, 1)
            dve.wait_ge(s_set_dve, 5)
            dve.tensor_scalar(up_i, down_i, -1.0, float((254 + SCALE_EXP) << 23), ALU.mult, ALU.add).then_inc(s_set_dve, 1)
            dve.wait_ge(s_set_dve, 6)
            dve.tensor_scalar(down_i, up_i, -1.0, float(254 << 23), ALU.mult, ALU.add).then_inc(s_set_dve, 1)
            for k in range(3):
                dve.tensor_scalar(vT[:, k], vT[:, k], up[:, k:k + 1], None, ALU.mult).then_inc(s_set_dve, 1)
                dve.tensor_scalar(w_hh_n[:, k], w_hh_n[:, k], up[:, k:k + 1], None, ALU.mult).then_inc(s_set_dve, 1)
            dve.wait_ge(s_w[3], 16)
            dve.wait_ge(s_w[4], 16)
            dve.tensor_tensor(bias_rz[:, :], bi[:, :], bh[:, :], ALU.add).then_inc(s_set_dve, 1)
            dve.tensor_tensor(bias_hn[:, :], bh[:, 2:3], up[:, 2:3], ALU.mult).then_inc(s_set_dve, 1)
            for k, tile in ((8, w_rel_s), (9, w_root_s), (10, b_rel_row)):
                dve.wait_ge(s_w[k], 16)
                dve.tensor_scalar(tile[:, :], tile[:, :], 0.5, None, ALU.mult).then_inc(s_half, 1)
            for l in range(L + 1):
                dve.wait_ge(s_set_act, 10 + l)
                hi, lo = (v_hi[:, l], v_lo[:, l]) if l < L else (u_hi[:, :, :], u_lo[:, :, :])
                dve.tensor_tensor(lo, (p_a, p_b)[l % 2][:, 0:3 * P].rearrange("p (k c) -> p k c", k=3), hi, ALU.subtract)\
                    .then_inc(s_set_dve, 1)

            def bn(src, g, st, done, src_done, value):
                ge(dve, src_done, value)
                for c in range(C):
                    last = dve.bn_stats(st[:, C * g + c], src[:, g, c])
                last.then_inc(done, 1)

            def art_steps(p):
                k0 = ART_STEPS * p

                def ts(dst, src, wait, a, c_, oa, ob=ALU.bypass):
                    ge(dve, art_step, k0 + wait)
                    dve.tensor_scalar(dst, src, a, c_, oa, ob).then_inc(art_step, 1)

                def tt(dst, i0, i1, wait, op):
                    ge(dve, art_step, k0 + wait)
                    dve.tensor_tensor(dst, i0, i1, op).then_inc(art_step, 1)
                return k0, ts, tt

            def slot(b, t):
                n = S * b + t
                if live(b):
                    ge(dve, r_ready, n + 1)
                    dve.scalar_tensor_tensor(out=t_s[:, t % 2], in0=p_hn[:, :], scalar=bias_hn[:, 0:1],
                                             in1=r_s[:, t % 2], op0=ALU.add, op1=ALU.mult).then_inc(t_done, 1)
                for m, u in following(b, t):
                    ge(dve, agg_hi_ready, S * m + u + 1)
                    dve.tensor_tensor(agg_lo[:, u % 2], p_agg[:, :], agg_hi[:, u % 2], ALU.subtract)\
                        .then_inc(agg_lo_ready, 1)
                if live(b):
                    ge(dve, gates_ps, 4 * n + 3)
                    ge(dve, t_done, n + 1)
                    dve.tensor_tensor(t_s[:, t % 2], p_in[:, :], t_s[:, t % 2], ALU.add).then_inc(t2_done, 1)
                for p, g in due(b, t, PRE_IN + 1, 1):
                    part = slice(C * g, C * g + C)
                    ge(dve, sumsq_done, G * p + g + 1)
                    dve.tensor_scalar(art[:, 0, part], sumsq[:, part], TINY_SQ, None, ALU.max).then_inc(art_max, 1)
                for p, g in due(b, t, PRE_MM + 1, 1):
                    part = slice(C * g, C * g + C)
                    ge(dve, sup_sq_done, G * p + g + 1)
                    dve.tensor_scalar(ball[:, 0, part], sup_sq[:, part], TINY_SQ, None, ALU.max).then_inc(ball_max, 1)
                for q, g in due(b, t, POST_CONV, -1):
                    ge(dve, conv_ps, G * q + g + 1)
                    ge(dve, out_stored[g], 16 * q)
                    dve.tensor_tensor(v4[:, g], p_b[:, :].rearrange("p (c d) -> p c d", c=C), graphs(b_rel_row),
                                      ALU.add).then_inc(conv_done, 1)
                for q in due_batch(b, t, POST_LN2, -1):
                    ln_dve(dve, st2, ln2, ln2_step, LN_STEPS, q, st2_done)
                for q in due_batch(b, t, POST_LN4, -1):
                    ln_dve(dve, st4, ln4, ln4_step, LN_STEPS, q, st4_done, EPS / 4)
                for q in due_batch(b, t, POST_LN3, -1):
                    ln_dve(dve, st3, ln3, ln3_step, LN3_STEPS, q, st3_done)
                    k0 = LN3_STEPS * q
                    dve.tensor_scalar(ln3[:, VAR], ln3[:, 4], 1.0 / P, None, ALU.mult).then_inc(ln3_step, 1)
                    ge(dve, ln3_step, k0 + 7)
                    dve.reciprocal(ln3[:, 9], ln3[:, VAR_EPS]).then_inc(ln3_step, 1)
                    ge(dve, ln3_step, k0 + 9)
                    dve.tensor_tensor(ln3[:, 9], ln3[:, 9], ln3[:, VAR], ALU.mult).then_inc(ln3_step, 1)
                    ge(dve, ln3_step, k0 + 10)
                    dve.tensor_scalar(ln3[:, 9], ln3[:, 9], EPS, None, ALU.add).then_inc(ln3_step, 1)
                for m, u in earlier(b, t, 1):
                    ge(dve, z_ready, S * m + u + 1)
                    ge(dve, d_ready, S * m + u + 1)
                    dve.tensor_tensor(d_s[:, u % 2], z_s[:, u % 2], d_s[:, u % 2], ALU.mult).then_inc(zd_done, 1)
                    ge(dve, zd_done, S * m + u + 1)
                    if u < G:
                        ge(dve, hT_ps, G * (m - 1) + u + 1)
                    dve.tensor_tensor(h_st[:, u % G], c_s[:, u % 2], d_s[:, u % 2], ALU.add).then_inc(h_done, 1)
                if live(b) and 2 <= t < SN + 2:
                    u = t - 2
                    ge(dve, nt_ps, SN * b + u + 1)
                    dve.tensor_copy(n_st[:, u % G].rearrange("p s c d -> p (s c d)"), p_nt[:, :]).then_inc(n_ready, 1)
                for q, g in due(b, t, POST_CONV, -1):
                    ge(dve, conv_done, G * q + g + 1)
                    dve.scalar_tensor_tensor(out=v4[:, g], in0=v4[:, g], scalar=0.0, in1=res[:, g],
                                             op0=ALU.max, op1=ALU.add).then_inc(v4_done, 1)
                    bn(v4, g, st4, st4_done, v4_done, G * q + g + 1)
                for q, g in due(b, t, POST_H, -1):
                    ge(dve, h2_ps, G * q + g + 1)
                    ge(dve, y_ps, G * q + g - 1)
                    dve.tensor_tensor(h2[:, g % 2], p_b[:, :].rearrange("p (c d) -> p c d", c=C), graphs(b2_row), ALU.add)\
                        .then_inc(h2b_done, 1)
                for p in due_batch(b, t, PRE_ART + 1, 1):
                    k0, ts, tt = art_steps(p)
                    ge(dve, art_norm, G * (p + 1))
                    ts(art[:, 2], art[:, 1], 0, ATANH_MAX, None, ALU.min)
                    dve.reciprocal(art[:, 6], art[:, 1]).then_inc(art_step, 1)
                    ts(art[:, 4], art[:, 2], 1, -1.0, 1.0, ALU.mult, ALU.add)
                    ts(art[:, 3], art[:, 2], 1, 1.0, None, ALU.add)
                    ge(dve, art_step, k0 + 3)
                    dve.reciprocal(art[:, 5], art[:, 4]).then_inc(art_step, 1)
                    tt(art[:, 8], art[:, 2], art[:, 2], 1, ALU.mult)
                    tt(art[:, 7], art[:, 3], art[:, 5], 5, ALU.mult)
                    ts(art[:, 9], art[:, 8], 6, 1.0 / SERIES[0], None, ALU.mult)
                    ts(art[:, 10], art[:, 2], 1, SERIES_BELOW, None, ALU.is_lt)
                    for i, k in enumerate(SERIES[1:]):
                        ge(dve, art_step, k0 + (9 + i if i else 8))
                        dve.scalar_tensor_tensor(out=art[:, 9], in0=art[:, 9], scalar=1.0 / k, in1=art[:, 8],
                                                 op0=ALU.add, op1=ALU.mult).then_inc(art_step, 1)
                    ts(art[:, 9], art[:, 9], 13, 1.0, None, ALU.add)
                for p in due_batch(b, t, PRE_ART + 2, 1):
                    k0, ts, tt = art_steps(p)
                    ge(dve, art_ln_done, p + 1)
                    ge(dve, art_step, k0 + 14)
                    dve.scalar_tensor_tensor(out=art[:, 5], in0=art[:, 11], scalar=0.5, in1=art[:, 6],
                                             op0=ALU.mult, op1=ALU.mult).then_inc(art_step, 1)
                    tt(art[:, 9], art[:, 9], art[:, 5], 15, ALU.subtract)
                    tt(art[:, 9], art[:, 9], art[:, 10], 16, ALU.mult)
                    tt(tan_scale[:, :], art[:, 9], art[:, 5], 17, ALU.add)
                for p in due_batch(b, t, PRE_BALL + 1, 1):
                    k0 = BALL_STEPS * p
                    ge(dve, ball_norm, G * (p + 1))
                    dve.reciprocal(ball[:, 3], ball[:, 1]).then_inc(ball_step, 1)
                    ge(dve, ball_tanh, p + 1)
                    ge(dve, ball_step, k0 + 1)
                    dve.scalar_tensor_tensor(out=ball[:, 3], in0=ball[:, 2], scalar=BALL_MAX, in1=ball[:, 3],
                                             op0=ALU.min, op1=ALU.mult).then_inc(ball_step, 1)
                for p, g in due(b, t, PRE_V, 1):
                    ge(dve, ball_step, BALL_STEPS * (p + 1))
                    for c in range(C):
                        last = dve.scalar_tensor_tensor(out=v1[:, g, c], in0=v1[:, g, c], scalar=col(ball[:, 3], g, c),
                                                        in1=x_in[:, g, c], op0=ALU.mult, op1=ALU.add)
                    last.then_inc(v1_done, 1)
                    bn(v1, g, st1, st1_done, v1_done, G * p + g + 1)
                for q, g in due(b, t, POST_H3, -1):
                    ge(dve, x3_ready, G * q + g + 1)
                    ge(dve, ln3_factor, G * q + g + 1)
                    ge(dve, agg3_ps, G * q + g - 1)
                    for c in range(C):
                        last = dve.scalar_tensor_tensor(out=h3[:, g % 2, c], in0=res[:, g, c], scalar=col(ln3[:, 10], g, c),
                                                        in1=gamma_row[:, :], op0=ALU.mult, op1=ALU.mult)
                    last.then_inc(h3g_done, 1)
                for q, g in due(b, t, POST_OUT, -1):
                    ge(dve, ln4_ready, G * q + g + 1)
                    for c in range(C):
                        last = dve.tensor_scalar(v4[:, g, c], v4[:, g, c], col(ln4[:, RSTD], g, c),
                                                 col(ln4[:, SHIFT], g, c), ALU.mult, ALU.add)
                    last.then_inc(out_ready, 1)
                if t == PRE_ART - 1:
                    if live(b - 1):
                        ge(dve, dinv_mid_done, b)
                        ge(dve, v3_done, G * (b - 1))
                        dve.tensor_copy(dinv_post[:, :], dinv_mid[:, :])\
                            .then_inc(dinv_post_done, 1)
                    if live(b):
                        ge(dve, dinv_pre_done, G * (b + 1))
                        ge(dve, dinv_post_done, b)
                        dve.tensor_copy(dinv_mid[:, :], dinv_pre[:, :])\
                            .then_inc(dinv_mid_done, 1)
                for p in due_batch(b, t, PRE_LN, 1):
                    ln_dve(dve, st1, ln1, ln1_step, LN_STEPS, p, st1_done)
                for p, g in due(b, t, PRE_IN, 1):
                    if g == 0:
                        ge(dve, dinv_pre_done, G * p)
                    ge(dve, adj_off_done, G * p + g + 1)
                    dve.tensor_reduce(degree[:, C * g:C * g + C], adj_off[:, g % 2], AX.X, ALU.add)\
                        .then_inc(degree_done, 1)
                if t >= S - G and live(b + 1):
                    g = t - (S - G)
                    ge(dve, agg_ps, S * b + t + 1)
                    ge(dve, adj_loaded[g], 16 * (b + 2))
                    dve.tensor_scalar(linked[:, g], adj_in[:, g].rearrange("p c j -> p (c j)"), 0.0, None,
                                      ALU.not_equal).then_inc(linked_ready, 1)
                for q, g in due(b, t, POST_Y, -1):
                    ge(dve, y_ps, G * q + g + 1)
                    for c in range(C):
                        last = dve.scalar_tensor_tensor(out=res[:, g, c], in0=p_a[:, P * c:P * c + P],
                                                        scalar=col(dinv_post, g, c), in1=res[:, g, c],
                                                        op0=ALU.mult, op1=ALU.add)
                    last.then_inc(v3_done, 1)
                    bn(res, g, st3, st3_done, v3_done, G * q + g + 1)
                for q, g in due(b, t, POST_V2, -1):
                    ge(dve, hT_ps, G * q + g + 1)
                    ge(dve, mask_in, 16 * (q + 1))
                    ge(dve, x1_post_in[g], 16 * (q + 1))
                    for c in range(C):
                        last = dve.scalar_tensor_tensor(out=res[:, g, c], in0=p_b[:, P * c:P * c + P],
                                                        scalar=col(mask_post, g, c), in1=x1_post[:, g, c],
                                                        op0=ALU.mult, op1=ALU.add)
                    last.then_inc(v2_done, 1)
                    bn(res, g, st2, st2_done, v2_done, G * q + g + 1)
            run(dve, slot)

        @block.tensor
        def _(pe):
            def turn(dst, src, n, identity=ident):
                for k in range(n):
                    last = pe.transpose(dst[:, P * k:P * k + P], src(k), identity[:, :])
                return last

            pe.wait_ge(s_const, 8)
            pe.wait_ge(s_w[0], 16)
            turn(p_hn, lambda k: w_ih_n[:, k], 3).then_inc(s_set_pe, 1)
            pe.wait_ge(s_w[1], 16)
            turn(p_r, lambda k: weight_n[:, k], C).then_inc(s_set_pe, 1)
            turn(p_in, lambda k: weight_n[:, C + k], L - C).then_inc(s_set_pe, 1)
            pe.wait_ge(s_w[5], 16)
            turn(p_z, lambda k: mask_n[:, :], 1).then_inc(s_set_pe, 1)
            pe.wait_ge(s_w[6], 16)
            pe.wait_ge(s_set_act, SET_MASK)
            turn(p_z[:, P:2 * P], lambda k: w2_n[:, :], 1).then_inc(s_set_pe, 1)
            pe.wait_ge(s_set_act, SET_W2)
            for k in range(3):
                pe.matmul((p_hn, p_r, p_in)[k][:, :], w_ihT[:, k], weightT[:, 0:W], start=True, stop=True)\
                    .then_inc(s_set_pe, 1)
            for k in range(3):
                last = pe.matmul(p_agg[:, P * k:P * k + P], w_ihT[:, k], weightT[:, W:L * P], start=True, stop=True)
            last.then_inc(s_set_pe, 1)
            pe.wait_ge(s_set_dve, 13)
            for l in range(L + 1):
                if l >= 2:
                    pe.wait_ge(s_set_dve, 15 + l - 1)
                src = (lambda k: vT[:, k, P * l:P * l + P]) if l < L else (lambda k: w_hh_n[:, k])
                turn((p_a, p_b)[l % 2], src, 3).then_inc(s_set_pe, 1)
            pe.wait_ge(s_set_dve, 15 + L + 1)
            for k in range(8, 13):
                pe.wait_ge(s_w[k], 16)
            pe.wait_ge(s_w[7], 16)
            pe.wait_ge(s_half, 3)

            reader = {"a": None, "b": None}

            def claim(b, bank):
                if reader[bank]:
                    s, per, off, c = reader[bank]
                    ge(pe, s, per * (b + off) + c)

            def read_by(b, bank, s, batch_off, g):
                reader[bank] = (s, G, batch_off, g + 1)

            def next_iteration():
                for k, v in reader.items():
                    if v:
                        reader[k] = (v[0], v[1], v[2] - 1, v[3])

            def split3(bank, hi, lo, xh, xl, start, stop, before_lo=None):
                pe.matmul(bank[:, :], hi, xh, start=start, stop=False)
                pe.matmul(bank[:, :], lo, xh, start=False, stop=False)
                if before_lo:
                    before_lo()
                return pe.matmul(bank[:, :], hi, xl, start=False, stop=stop)

            def off_of(first, g, ahead):
                return ahead - (first + g) // S

            def aggregate(b, t):
                g = t % G
                n_old = n_first if t < G else n_st
                if t < G:
                    ge(pe, n_first_lo, G * b + g + 1)
                    ge(pe, linked_ready, G * b + g + 1)
                else:
                    ge(pe, n_ready, SN * b + t - G + 1)
                ge(pe, agg_lo_ready, S * b + t)
                for c in range(C):
                    for part in range(2):
                        last = pe.matmul(p_agg[:, P * c:P * c + P], n_old[:, g, part, c], linked[:, g, P * c:P * c + P],
                                         start=(part == 0), stop=(part == 1))
                last.then_inc(agg_ps, 1)

            def slot(b, t):
                g0, l, n = t % G, t // G, S * b + t
                if live(b):
                    if l == 0:
                        ge(pe, hl_first_ready, G * b + g0 + 1)
                        hh, hl = hh_first[:, g0], hl_first[:, g0]
                    else:
                        ge(pe, hl_ready, SN * b + t - G + 1)
                        hh, hl = hh_st[:, g0], hl_st[:, g0]
                    ah, al = agg_hi[:, t % 2], agg_lo[:, t % 2]
                    ge(pe, t_done, n)
                    split3(p_hn, u_hi[:, 2], u_lo[:, 2], hh, hl, True, True).then_inc(gates_ps, 1)
                    ge(pe, r_ready, n)
                    split3(p_r, u_hi[:, 0], u_lo[:, 0], hh, hl, True, False)
                    ge(pe, agg_hi_ready, n + 1)
                    split3(p_r, v_hi[:, l, 0], v_lo[:, l, 0], ah, al, False, True,
                           lambda: ge(pe, agg_lo_ready, n + 1)).then_inc(gates_ps, 1)
                for p, g in due(b, t, PRE_MM, 1):
                    ge(pe, x_tan_ready, G * p + g + 1)
                    claim(b, "a")
                    for c in range(C):
                        last = pe.matmul(p_a[:, P * c:P * c + P], adjT_pre[:, g, c], x_tan[:, g % 2, c],
                                         start=True, stop=True)
                    last.then_inc(sup_ps, 1)
                    read_by(b, "a", sup_ready, off_of(PRE_MM, g, 1), g)
                for p, g in due(b, t, PRE_X1T, 1):
                    ge(pe, x1_ready, G * p + g + 1)
                    claim(b, "a")
                    turn(p_a, lambda c: x1_pre[:, g, c], C).then_inc(x1T_ps, 1)
                    read_by(b, "a", hh_first_ready, off_of(PRE_X1T, g, 1), g)
                for q, g in due(b, t, POST_CONV, -1):
                    ge(pe, h3T_ready, G * q + g + 1)
                    ge(pe, agg3_ready, G * q + min(g + 2, G))
                    claim(b, "b")
                    for c in range(C):
                        o = p_b[:, P * c:P * c + P]
                        pe.matmul(o, agg3[:, g % 2, P * c:P * c + P], w_rel_s[:, :], start=True, stop=False)
                        last = pe.matmul(o, h3T[:, g % 2, P * c:P * c + P], w_root_s[:, :], start=False, stop=True)
                    last.then_inc(conv_ps, 1)
                    read_by(b, "b", conv_done, off_of(POST_CONV, g, -1), g)
                for q, g in due(b, t, POST_X2T, -1):
                    ge(pe, x2_ready, G * q + g + 1)
                    claim(b, "b")
                    turn(p_b, lambda c: res[:, g, c], C).then_inc(x2T_ps, 1)
                    read_by(b, "b", x2T_ready, off_of(POST_X2T, g, -1), g)
                for m, u in following(b, t):
                    aggregate(m, u)
                if live(b):
                    ge(pe, t2_done, n)
                    split3(p_in, v_hi[:, l, 2], v_lo[:, l, 2], ah, al, True, True).then_inc(gates_ps, 1)
                    ge(pe, z_ready, n)
                    split3(p_z, u_hi[:, 1], u_lo[:, 1], hh, hl, True, False)
                    split3(p_z, v_hi[:, l, 1], v_lo[:, l, 1], ah, al, False, True).then_inc(gates_ps, 1)
                if live(b) and 2 <= t < SN + 2:
                    u = t - 2
                    ge(pe, hl_ready, SN * b + u + 1)
                    ge(pe, n_ready, SN * b + u)
                    turn(p_nt, lambda c: hh_st[:, u % G, P * c:P * c + P], C, ident16)
                    turn(p_nt[:, W:2 * W], lambda c: hl_st[:, u % G, P * c:P * c + P], C, ident16).then_inc(nt_ps, 1)
                for p, g in due(b, t, PRE_IN, 1):
                    ge(pe, adj_loaded[g], 16 * (p + 1))
                    claim(b, "a")
                    turn(p_a, lambda c: adj_in[:, g, c], C).then_inc(adjT_ps, 1)
                    read_by(b, "a", adjT_ready, off_of(PRE_IN, g, 1), g)
                for q, g in due(b, t, POST_V2, -1):
                    ge(pe, h_done, S * q + S - G + g + 1)
                    claim(b, "b")
                    turn(p_b, lambda c: h_st[:, g, P * c:P * c + P], C).then_inc(hT_ps, 1)
                    read_by(b, "b", v2_done, off_of(POST_V2, g, -1), g)
                for q, g in due(b, t, POST_H, -1):
                    ge(pe, x2T_ready, G * q + g + 1)
                    claim(b, "b")
                    for c in range(C):
                        last = pe.matmul(p_b[:, P * c:P * c + P], x2T[:, g % 2, P * c:P * c + P], w2T[:, :],
                                         start=True, stop=True)
                    last.then_inc(h2_ps, 1)
                    read_by(b, "b", h2b_done, off_of(POST_H, g, -1), g)
                for q, g in due(b, t, POST_Y, -1):
                    ge(pe, h2s_ready, G * q + g + 1)
                    ge(pe, adjT_post_in[g], 16 * (q + 1))
                    claim(b, "a")
                    for c in range(C):
                        last = pe.matmul(p_a[:, P * c:P * c + P], adjT_post[:, g, c], h2[:, g % 2, c],
                                         start=True, stop=True)
                    last.then_inc(y_ps, 1)
                    read_by(b, "a", v3_done, off_of(POST_Y, g, -1), g)
                for q, g in due(b, t, POST_AGG, -1):
                    ge(pe, h3_ready, G * q + g + 1)
                    claim(b, "a")
                    turn(p_a, lambda c: h3[:, g % 2, c], C).then_inc(h3T_ps, 1)
                    read_by(b, "a", h3T_ready, off_of(POST_AGG, g, -1), g)
                    claim(b, "b")
                    for c in range(C):
                        last = pe.matmul(p_b[:, P * c:P * c + P], h3[:, g % 2, c], adjT_post[:, g, c],
                                         start=True, stop=True)
                    last.then_inc(agg3_ps, 1)
                    read_by(b, "b", agg3_ready, off_of(POST_AGG, g, -1), g)
                if t == S - 1:
                    next_iteration()
            run(pe, slot)


_INS = ['x', 'adj', 'nodemask', 'L1_gnn_weight', 'L1_gnn_w_ih', 'L1_gnn_w_hh', 'L1_gnn_b_ih', 'L1_gnn_b_hh',
        'L2_gnn_W', 'L2_gnn_b', 'L3_gnn_W_rel', 'L3_gnn_b_rel', 'L3_gnn_W_root', 'L3_gnn_ln_gamma', 'L3_gnn_ln_beta']
_OUTS = [((128, 128, 128), 'float32')]


def kernel(**inputs):
    import numpy as _np
    import concourse.bacc as _bacc
    from concourse import mybir as _mybir
    from concourse.bass_utils import run_bass_kernel_spmd as _run

    nc = _bacc.Bacc("TRN2", target_bir_lowering=False, num_devices=1)
    arrays, args = {}, []
    for name in _INS:
        a = _np.ascontiguousarray(inputs[name])
        arrays[f"in_{name}_dram"] = a
        args.append(nc.dram_tensor(f"in_{name}_dram", a.shape, _mybir.dt.from_np(a.dtype), kind="ExternalInput").ap())
    for i, (shape, dtype) in enumerate(_OUTS):
        dt = _mybir.dt.from_np(_np.dtype(dtype))
        args.append(nc.dram_tensor(f"out_{i}_dram", shape, dt, kind="ExternalOutput").ap())
    build(nc, *args)
    r = _run(nc, [arrays], core_ids=[0])
    got = tuple(r.results[0][f"out_{i}_dram"] for i in range(len(_OUTS)))
    return got[0]
```

```python
from contextlib import ExitStack

import concourse.bass as bass
from concourse import mybir

F32 = mybir.dt.float32
F16 = mybir.dt.float16
I32 = mybir.dt.int32
ALU = mybir.AluOpType
ACT = mybir.ActivationFunctionType
AX = mybir.AxisListType

P = 128
C = 4
G = 4
W = C * P
BG = G * C

EPS = 1e-5
TINY_SQ = 1e-30
ATANH_MAX = 1.0 - 1e-7
BALL_MAX = 1.0 - 0.004
SERIES_BELOW = 0.25
SERIES = (11, 9, 7, 5, 3)
SCALE_EXP = 8

PRE_IN = 1
PRE_OFF = 1
PRE_DEG = 1
PRE_SQ = 0
PRE_NORM_MAX = 0
PRE_NORM = 1
PRE_ART_SERIES = 5
PRE_ART_LN = 6
PRE_ART_END = 6
PRE_XT = 7
PRE_MM = 8
PRE_SUPSQ = 8
PRE_BALL_MAX = 9
PRE_BALL_NORM = 9
PRE_BALL = 12
PRE_BALL_END = 12
PRE_V = 12
PRE_V_BN = 13
PRE_LN = 16
PRE_LN_POW = 17
PRE_X1 = 17
PRE_X1_HI = 17
PRE_X1_LO = 18
PRE_X1T = 18
PRE_X1T_LO = 18
DINV_MOVE = 3
PRE_DINV = 12
POST_V2 = 0
POST_V2_BN = 0
POST_LN2 = 4
POST_LN2_POW = 4
POST_X2 = 5
POST_X2T = 6
POST_H = 6
POST_H_SCALED = 8
POST_Y = 8
POST_Y_BN = 8
POST_LN3 = 12
POST_LN3_POW = 13
POST_FACTOR = 13
POST_X3 = 13
POST_H3 = 14
POST_H3_SHIFTED = 15
POST_AGG_T = 15
POST_AGG = 15
POST_CONV = 17
POST_V4 = 17
POST_V4_BN = 17
POST_LN4 = 22
POST_LN4_POW = 24
POST_OUT = 26

ART_STEPS = 18
BALL_STEPS = 2
LN_STEPS = 7
LN3_STEPS = 11


def build(nc, x, adj, nodemask, weight, w_ih, w_hh, b_ih, b_hh, w2, b2, w_rel, b_rel, w_root, gamma, beta, out):
    NB = x.shape[0] // BG
    L = weight.shape[0]
    S = L * G
    SN = S - G
    LOOP0, LOOP1 = 2, NB - 2

    with ExitStack() as ctx:
        def sb(name, shape, dt=F32):
            return ctx.enter_context(nc.sbuf_tensor(name, shape, dt))

        def pb(name, dt=F32):
            return ctx.enter_context(nc.psum_tensor(name, [P, 2048 // mybir.dt.size(dt)], dt))

        def sem(name):
            return ctx.enter_context(nc.semaphore(name))

        def sems(name, n):
            return [sem(f"{name}{i}") for i in range(n)]

        ident = sb("ident", [P, P])
        offdiag = sb("offdiag", [P, P])
        half16 = sb("half16", [P, 2, BG])
        w_hh_n = sb("w_hh_n", [P, 3, P])
        v_hi = sb("v_hi", [P, L, 3, P], F16)
        v_lo = sb("v_lo", [P, L, 3, P], F16)
        u_hi = sb("u_hi", [P, 3, P], F16)
        u_lo = sb("u_lo", [P, 3, P], F16)
        rowmax = sb("rowmax", [P, 3, 3])
        up = sb("up", [P, 3])
        down = sb("down", [P, 3])
        bi = sb("bi", [P, 3])
        bh = sb("bh", [P, 3])
        bias_rz = sb("bias_rz", [P, 3])
        bias_hn = sb("bias_hn", [P, 1])
        w2_n = sb("w2_n", [P, P])
        w2T = sb("w2T", [P, P])
        b2_row = sb("b2_row", [P, P])
        w_rel_s = sb("w_rel_s", [P, P])
        w_root_s = sb("w_root_s", [P, P])
        b_rel_row = sb("b_rel_row", [P, P])
        gamma_row = sb("gamma_row", [P, P])
        beta_row = sb("beta_row", [P, P])
        mask_n = sb("mask_n", [P, P])
        maskT = sb("maskT", [P, P])

        x_in = sb("x_in", [P, G, C, P])
        adj_in = sb("adj_in", [P, G, C, P])
        adj_off = sb("adj_off", [P, 2, C, P])
        adjT_pre = sb("adjT_pre", [P, G, C, P])
        x_tan = sb("x_tan", [P, 2, C, P])
        v1 = sb("v1", [P, G, C, P])
        x1_pre = sb("x1_pre", [P, G, C, P])
        act_junk = sb("act_junk", [P, C, P], F16)
        sumsq = sb("sumsq", [P, BG])
        art = sb("art", [P, 12, BG])
        tan_scale = sb("tan_scale", [P, BG])
        sup_sq = sb("sup_sq", [P, BG])
        ball = sb("ball", [P, 4, BG])
        degree = sb("degree", [P, BG])
        dinv_pre = sb("dinv_pre", [P, BG])
        dinv_mid = sb("dinv_mid", [P, BG])
        dinv_post = sb("dinv_post", [P, BG])
        st1, st2, st3, st4 = (sb(f"st{i}", [P, BG, 6]) for i in range(1, 5))
        ln1, ln2, ln4 = (sb(f"ln{i}", [P, 9, BG]) for i in (1, 2, 4))
        ln3 = sb("ln3", [P, 11, BG])

        linked = sb("linked", [P, G, W], F16)
        n_first = sb("n_first", [P, G, 2, C, P], F16)
        h_first = sb("h_first", [P, G, W])
        hh_first = sb("hh_first", [P, G, W], F16)
        hl_first = sb("hl_first", [P, G, W], F16)
        n_st = sb("n_st", [P, G, 2, C, P], F16)
        h_st = sb("h_st", [P, G, W])
        hh_st = sb("hh_st", [P, G, W], F16)
        hl_st = sb("hl_st", [P, G, W], F16)
        agg_hi = sb("agg_hi", [P, 2, W], F16)
        agg_lo = sb("agg_lo", [P, 2, W], F16)
        r_s = sb("r_s", [P, 2, W])
        z_s = sb("z_s", [P, 2, W])
        t_s = sb("t_s", [P, 2, W])
        c_s = sb("c_s", [P, 2, W])
        d_s = sb("d_s", [P, 2, W])

        adjT_mid = sb("adjT_mid", [P, G, C, P])
        adjT_post = sb("adjT_post", [P, G, C, P])
        x1_post = sb("x1_post", [P, G, C, P])
        mask_post = sb("mask_post", [P, BG])
        res = sb("res", [P, G, C, P])
        x2T = sb("x2T", [P, 2, W])
        h2 = sb("h2", [P, 2, C, P])
        h3 = sb("h3", [P, 2, C, P])
        h3T = sb("h3T", [P, 2, W])
        agg3 = sb("agg3", [P, 2, W])
        v4 = sb("v4", [P, G, C, P])

        res_flat = res[:, :, :, :].rearrange("p g c d -> p (g c d)")
        w_ih_n = res_flat[:, 0:3 * P].rearrange("p (k c) -> p k c", k=3)
        w_ihT = res_flat[:, 3 * P:6 * P].rearrange("p (k c) -> p k c", k=3)
        weight_n = res_flat[:, 6 * P:(6 + L) * P].rearrange("p (l c) -> p l c", l=L)
        weightT = res_flat[:, (6 + L) * P:(6 + 2 * L) * P]
        vT = v4[:, :, :, :].rearrange("p g c d -> p (g c d)")[:, 0:3 * L * P].rearrange("p (k c) -> p k c", k=3)

        p_hn, p_r, p_in, p_z, p_agg = (pb(f"p_{n}") for n in ("hn", "r", "in", "z", "agg"))
        p_nt = pb("p_nt")
        p_a, p_b = pb("p_a"), pb("p_b")

        s_w = sems("s_w", 14)
        s_const = sem("s_const")
        s_set_pe = sem("s_set_pe")
        s_set_dve = sem("s_set_dve")
        s_half = sem("s_half")
        s_set_act = sem("s_set_act")
        x_loaded, adj_loaded = sems("x_loaded", G), sems("adj_loaded", G)
        adjT_mid_in, adjT_post_in, x1_post_in = sems("adjT_mid_in", G), sems("adjT_post_in", G), sems("x1_post_in", G)
        mask_in = sem("mask_in")
        out_stored = sems("out_stored", G)
        names = """sumsq_done adj_off_done degree_done adjT_ps adjT_ready art_step art_ln_done dinv_pre_done dinv_mid_done
            dinv_post_done x_tan_ready sup_ps sup_ready sup_sq_done ball_step v1_done st1_done ln1_step x1_ready
            n_first_hi n_first_lo x1T_ps h_first_ready hh_first_ready hl_first_ready linked_ready
            agg_ps agg_hi_ready agg_lo_ready gates_ps r_ready t_done t2_done cand_ready z_ready d_ready zd_done h_done
            hh_ready hl_ready nt_ps n_hi_ready n_ready
            hT_ps v2_done st2_done ln2_step x2_ready x2T_ps x2T_ready h2_ps h2b_done h2s_ready y_ps v3_done st3_done
            ln3_step x3_ready h3g_done h3_ready h3T_ps agg3_ps h3T_ready agg3_ready conv_ps conv_done v4_done
            st4_done ln4_step out_ready
            art_norm art_max ball_max ball_norm ball_tanh ln1_pow ln2_pow ln3_pow ln4_pow
            ln1_ready ln2_ready ln3_ready ln3_factor ln4_ready""".split()
        (sumsq_done, adj_off_done, degree_done, adjT_ps, adjT_ready, art_step, art_ln_done, dinv_pre_done, dinv_mid_done,
         dinv_post_done, x_tan_ready, sup_ps, sup_ready, sup_sq_done, ball_step, v1_done, st1_done, ln1_step, x1_ready,
         n_first_hi, n_first_lo, x1T_ps, h_first_ready, hh_first_ready, hl_first_ready, linked_ready,
         agg_ps, agg_hi_ready, agg_lo_ready, gates_ps, r_ready, t_done, t2_done, cand_ready, z_ready, d_ready,
         zd_done, h_done, hh_ready, hl_ready, nt_ps, n_hi_ready, n_ready,
         hT_ps, v2_done, st2_done, ln2_step, x2_ready, x2T_ps, x2T_ready, h2_ps, h2b_done, h2s_ready, y_ps, v3_done,
         st3_done, ln3_step, x3_ready, h3g_done, h3_ready, h3T_ps, agg3_ps, h3T_ready, agg3_ready, conv_ps, conv_done,
         v4_done, st4_done, ln4_step, out_ready,
         art_norm, art_max, ball_max, ball_norm, ball_tanh, ln1_pow, ln2_pow, ln3_pow, ln4_pow,
         ln1_ready, ln2_ready, ln3_ready, ln3_factor, ln4_ready) = (sem(n) for n in names)

        def ge(eng, s, value):
            if not isinstance(value, int) or value > 0:
                eng.wait_ge(s, value)

        def live(batch):
            return not isinstance(batch, int) or 0 <= batch < NB

        def due(b, t, first, ahead):
            for g in range(G):
                if (first + g) % S == t:
                    batch = b + ahead - (first + g) // S
                    if live(batch):
                        yield batch, g

        def due_batch(b, t, first, ahead):
            batch = b + ahead - first // S
            return [batch] if first % S == t and live(batch) else []

        def earlier(b, t, back):
            batch, slot = (b, t - back) if t >= back else (b - 1, t - back + S)
            return [(batch, slot)] if live(batch) else []

        def following(b, t):
            batch, slot = (b, t + 1) if t < S - 1 else (b + 1, 0)
            return [(batch, slot)] if live(batch) else []

        def run(eng, slot, setup=None):
            for b in range(-1, LOOP0):
                for t in range(S):
                    if setup and b == -1:
                        setup(t)
                    slot(b, t)
            with eng.Fori(LOOP0, LOOP1) as b:
                for t in range(S):
                    slot(b, t)
            for b in range(LOOP1, NB + 2):
                for t in range(S):
                    slot(b, t)

        def graphs(row):
            return row[:, :].unsqueeze(1).broadcast_to([P, C, P])

        def columns(small, g):
            return small[:, C * g:C * g + C].unsqueeze(2).broadcast_to([P, C, P])

        def col(small, g, c):
            return small[:, C * g + c:C * g + c + 1]

        NEG_MEAN, VAR, RSTD, SHIFT, VAR_EPS = 0, 5, 6, 7, 8

        def ln_dve(dve, st, ln, step, steps, batch, st_done, used, eps=EPS):
            me, mo, qe, qo = st[:, :, 1], st[:, :, 4], st[:, :, 2], st[:, :, 5]
            ge(dve, used, G * batch)
            ge(dve, st_done, G * batch + G)
            dve.tensor_tensor(ln[:, 1], me, mo, ALU.subtract).then_inc(step, 1)
            dve.tensor_tensor(ln[:, 0], me, mo, ALU.add).then_inc(step, 1)
            dve.tensor_tensor(ln[:, 2], qe, qo, ALU.add).then_inc(step, 1)
            ge(dve, step, steps * batch + 1)
            dve.tensor_tensor(ln[:, 3], ln[:, 1], ln[:, 1], ALU.mult).then_inc(step, 1)
            ge(dve, step, steps * batch + 2)
            dve.tensor_scalar(ln[:, NEG_MEAN], ln[:, 0], -0.5, None, ALU.mult).then_inc(step, 1)
            ge(dve, step, steps * batch + 4)
            dve.scalar_tensor_tensor(out=ln[:, 4], in0=ln[:, 3], scalar=P / 4.0, in1=ln[:, 2],
                                     op0=ALU.mult, op1=ALU.add).then_inc(step, 1)
            ge(dve, step, steps * batch + 6)
            dve.tensor_scalar(ln[:, VAR_EPS], ln[:, 4], 1.0 / P, eps, ALU.mult, ALU.add).then_inc(step, 1)

        def ln_pool(pool, ln, step, steps, batch, g, powered, done):
            part = slice(C * g, C * g + C)
            ge(pool, step, steps * (batch + 1))
            pool.tensor_tensor(ln[:, RSTD, part], ln[:, VAR_EPS, part], half16[:, 1, part], ALU.pow).then_inc(powered, 1)
            ge(pool, powered, G * batch + g + 1)
            pool.tensor_tensor(ln[:, SHIFT, part], ln[:, NEG_MEAN, part], ln[:, RSTD, part], ALU.mult).then_inc(done, 1)

        SET_TURN, SET_ROWS, SET_SCALE, SET_SPLIT = 2, 4, 5, 6
        SET_MASK, SET_W2, SET_V = 4, 5, 9

        block = ctx.enter_context(nc.Block())

        @block.sync
        def _(sp):
            def load_x(at, g):
                src = x[bass.ds(at, C), :, :].rearrange("c n d -> n c d")
                sp.dma_start(x_in[:, g], src).then_inc(x_loaded[g], 16)

            def load_adj(at, g):
                src = adj[bass.ds(at, C), :, :].rearrange("c i j -> i c j")
                sp.dma_start(adj_in[:, g], src).then_inc(adj_loaded[g], 16)

            for g in range(G):
                load_x(C * g, g)
                load_adj(C * g, g)
            loads = [
                (w_ih_n[:, :, :], w_ih.rearrange("(k p) c -> p k c", p=P)),
                (weight_n[:, :, :], weight.rearrange("l d c -> d l c")),
                (w_hh_n[:, :, :], w_hh.rearrange("(k p) c -> p k c", p=P)),
                (bi[:, :], b_ih.rearrange("(k p) -> p k", p=P)),
                (bh[:, :], b_hh.rearrange("(k p) -> p k", p=P)),
                (mask_n[:, :], nodemask),
                (w2_n[:, :], w2),
                (b2_row[:, :], b2.partition_broadcast(P)),
                (w_rel_s[:, :], w_rel),
                (w_root_s[:, :], w_root),
                (b_rel_row[:, :], b_rel.partition_broadcast(P)),
                (gamma_row[:, :], gamma.partition_broadcast(P)),
                (beta_row[:, :], beta.partition_broadcast(P)),
            ]
            for (dst, src), s in zip(loads, s_w):
                sp.dma_start(dst, src, allow_slow_non_contiguous=True).then_inc(s, 16)

            def counts(*values):
                return [v if isinstance(v, int) else sp.compute_val(v) for v in values]

            def slot(b, t):
                for q, g in due(b, t, POST_OUT, -1):
                    at, rows = counts(q * BG + C * g, G * q + g + 1)
                    ge(sp, out_ready, rows)
                    dst = out[bass.ds(at, C), :, :].rearrange("c n d -> n c d")
                    sp.dma_start(dst, v4[:, g]).then_inc(out_stored[g], 16)
                if t == 5 and live(b):
                    at, read = counts(b * BG, G * b)
                    ge(sp, s_set_act, SET_MASK)
                    ge(sp, v2_done, read)
                    sp.dma_start(mask_post[:, :], maskT[:, bass.ds(at, BG)]).then_inc(mask_in, 16)
                    for g in range(G):
                        x1_there, = counts(G * b + g + 1)
                        ge(sp, x1_ready, x1_there)
                        sp.dma_start(x1_post[:, g], x1_pre[:, g]).then_inc(x1_post_in[g], 16)
                if t >= S - G - 1 and t < S - 1 and live(b + 2):
                    g = t - (S - G - 1)
                    at, read = counts((b + 2) * BG + C * g, G * (b + 1) + g + 1)
                    ge(sp, v1_done, read)
                    load_x(at, g)
                if t >= S - G:
                    g = t - (S - G)
                    if live(b + 2):
                        at, read = counts((b + 2) * BG + C * g, G * (b + 1) + g + 1)
                        ge(sp, linked_ready, read)
                        load_adj(at, g)
                    if live(b):
                        read, there = counts(G * (b - 1) + g + 1, 16 * (b + 1))
                        ge(sp, agg3_ps, read)
                        ge(sp, adjT_mid_in[g], there)
                        sp.dma_start(adjT_post[:, g], adjT_mid[:, g]).then_inc(adjT_post_in[g], 16)
                    if live(b + 1):
                        moved, there = counts(16 * (b + 1), G * (b + 1) + g + 1)
                        ge(sp, adjT_post_in[g], moved)
                        ge(sp, adjT_ready, there)
                        sp.dma_start(adjT_mid[:, g], adjT_pre[:, g]).then_inc(adjT_mid_in[g], 16)
            run(sp, slot)
            for g in range(G):
                sp.wait_ge(out_stored[g], 16 * NB)

        @block.gpsimd
        def _(pool):
            pool.memset(ident[:, :], 0.0).then_inc(s_const, 1)
            pool.memset(offdiag[:, :], 1.0).then_inc(s_const, 1)
            pool.memset(half16[:, 0], 0.5).then_inc(s_const, 1)
            pool.memset(half16[:, 1], -0.5).then_inc(s_const, 1)
            pool.wait_ge(s_const, 4)
            for tile, fill in ((ident, 1.0), (offdiag, 0.0)):
                pool.affine_select(out=tile[:, :], in_=tile[:, :], compare_op=ALU.not_equal, fill=fill, base=0,
                                   pattern=[[-1, P]], channel_multiplier=1).then_inc(s_const, 1)
            pool.wait_ge(s_const, 6)

            def slot(b, t):
                for m, u in earlier(b, t, 1):
                    h_old = h_first if u < G else h_st
                    ge(pool, cand_ready, S * m + u + 1)
                    pool.tensor_tensor(d_s[:, u % 2], h_old[:, u % G], c_s[:, u % 2], ALU.subtract).then_inc(d_ready, 1)
                for q, g in due(b, t, POST_H3_SHIFTED, -1):
                    ge(pool, h3g_done, G * q + g + 1)
                    pool.tensor_tensor(h3[:, g % 2], h3[:, g % 2], graphs(beta_row), ALU.add).then_inc(h3_ready, 1)
                for p, g in due(b, t, PRE_LN_POW, 1):
                    ln_pool(pool, ln1, ln1_step, LN_STEPS, p, g, ln1_pow, ln1_ready)
                for p, g in due(b, t, PRE_OFF, 1):
                    ge(pool, adj_loaded[g], 16 * (p + 1))
                    ge(pool, degree_done, G * p + g - 1)
                    pool.tensor_tensor(adj_off[:, g % 2], adj_in[:, g], graphs(offdiag), ALU.mult)\
                        .then_inc(adj_off_done, 1)
                for q, g in due(b, t, POST_H_SCALED, -1):
                    ge(pool, dinv_post_done, q + 1)
                    ge(pool, h2b_done, G * q + g + 1)
                    pool.tensor_tensor(h2[:, g % 2], h2[:, g % 2], columns(dinv_post, g), ALU.mult)\
                        .then_inc(h2s_ready, 1)
                for q, g in due(b, t, POST_LN4_POW, -1):
                    ln_pool(pool, ln4, ln4_step, LN_STEPS, q, g, ln4_pow, ln4_ready)
                for p, g in due(b, t, PRE_DINV, 1):
                    part = slice(C * g, C * g + C)
                    ge(pool, degree_done, G * p + g + 1)
                    ge(pool, dinv_mid_done, p)
                    pool.tensor_tensor(dinv_pre[:, part], degree[:, part], half16[:, 1, part], ALU.pow)\
                        .then_inc(dinv_pre_done, 1)
                for q, g in due(b, t, POST_LN3_POW, -1):
                    ln_pool(pool, ln3, ln3_step, LN3_STEPS, q, g, ln3_pow, ln3_ready)
                for p, g in due(b, t, PRE_XT, 1):
                    ge(pool, art_step, ART_STEPS * (p + 1))
                    ge(pool, sup_ps, G * p + g - 1)
                    pool.tensor_tensor(x_tan[:, g % 2], x_in[:, g], columns(tan_scale, g), ALU.mult)\
                        .then_inc(x_tan_ready, 1)
                for p, g in due(b, t, PRE_X1_LO, 1):
                    ge(pool, n_first_hi, G * p + g + 1)
                    pool.tensor_tensor(n_first[:, g, 1], x1_pre[:, g], n_first[:, g, 0], ALU.subtract)\
                        .then_inc(n_first_lo, 1)
                for q, g in due(b, t, POST_FACTOR, -1):
                    part = slice(C * g, C * g + C)
                    ge(pool, ln3_step, LN3_STEPS * (q + 1))
                    pool.tensor_tensor(ln3[:, 10, part], ln3[:, 9, part], half16[:, 1, part], ALU.pow)\
                        .then_inc(ln3_factor, 1)
                for m, u in earlier(b, t, 2):
                    if u < SN:
                        ge(pool, hh_ready, SN * m + u + 1)
                        pool.tensor_tensor(hl_st[:, u % G], h_st[:, u % G], hh_st[:, u % G], ALU.subtract)\
                            .then_inc(hl_ready, 1)
                for q, g in due(b, t, POST_LN2_POW, -1):
                    ln_pool(pool, ln2, ln2_step, LN_STEPS, q, g, ln2_pow, ln2_ready)
                for p, g in due(b, t, PRE_X1T_LO, 1):
                    ge(pool, hh_first_ready, G * p + g + 1)
                    pool.tensor_tensor(hl_first[:, g], h_first[:, g], hh_first[:, g], ALU.subtract)\
                        .then_inc(hl_first_ready, 1)
                for p, g in due(b, t, PRE_BALL_NORM, 1):
                    part = slice(C * g, C * g + C)
                    ge(pool, ball_max, G * p + g + 1)
                    pool.tensor_tensor(ball[:, 1, part], ball[:, 0, part], half16[:, 0, part], ALU.pow)\
                        .then_inc(ball_norm, 1)
                for p, g in due(b, t, PRE_NORM, 1):
                    part = slice(C * g, C * g + C)
                    ge(pool, art_max, G * p + g + 1)
                    pool.tensor_tensor(art[:, 1, part], art[:, 0, part], half16[:, 0, part], ALU.pow).then_inc(art_norm, 1)
            run(pool, slot)

        @block.scalar
        def _(act):
            def setup(t):
                if t == SET_TURN:
                    act.wait_ge(s_set_pe, 1)
                    act.activation(w_ihT[:, :, :].rearrange("p k c -> p (k c)"), p_hn[:, 0:3 * P], ACT.Copy).then_inc(s_set_act, 1)
                    act.wait_ge(s_set_pe, 2)
                    act.activation(weightT[:, 0:W], p_r[:, :], ACT.Copy).then_inc(s_set_act, 1)
                    act.wait_ge(s_set_pe, 3)
                    act.activation(weightT[:, W:L * P], p_in[:, 0:L * P - W], ACT.Copy).then_inc(s_set_act, 1)
                    act.wait_ge(s_set_pe, 4)
                    act.activation(maskT[:, :], p_z[:, 0:P], ACT.Copy).then_inc(s_set_act, 1)
                    act.wait_ge(s_set_pe, 5)
                    act.activation(w2T[:, :], p_z[:, P:2 * P], ACT.Copy).then_inc(s_set_act, 1)
                if t == SET_ROWS:
                    for k in range(3):
                        act.wait_ge(s_set_pe, 6 + k)
                        act.activation(vT[:, k, 0:W], (p_hn, p_r, p_in)[k][:, :], ACT.Copy).then_inc(s_set_act, 1)
                    act.wait_ge(s_set_pe, 9)
                    act.activation(vT[:, :, W:L * P], p_agg[:, 0:3 * P].rearrange("p (k c) -> p k c", k=3), ACT.Copy)\
                        .then_inc(s_set_act, 1)
                l = t - SET_SPLIT
                if 0 <= l <= L:
                    act.wait_ge(s_set_pe, 10 + l)
                    hi = v_hi[:, l] if l < L else u_hi[:, :, :]
                    act.activation(hi, (p_hn, p_r)[l % 2][:, 0:3 * P].rearrange("p (k c) -> p k c", k=3), ACT.Copy)\
                        .then_inc(s_set_act, 1)

            def apply(dst, src, ln, g, done):
                for c in range(C):
                    last = act.activation(dst[:, g, c], src[:, g, c], ACT.Identity, bias=col(ln[:, SHIFT], g, c),
                                          scale=col(ln[:, RSTD], g, c))
                last.then_inc(done, 1)

            def slot(b, t):
                if live(b):
                    ge(act, gates_ps, 4 * (S * b + t) + 2)
                    act.activation(r_s[:, t % 2], p_r[:, :], ACT.Sigmoid, bias=bias_rz[:, 0:1], scale=down[:, 0:1])\
                        .then_inc(r_ready, 1)
                for m, u in following(b, t):
                    ge(act, agg_ps, S * m + u + 1)
                    act.activation(agg_hi[:, u % 2], p_agg[:, :], ACT.Copy).then_inc(agg_hi_ready, 1)
                for q, g in due(b, t, POST_X2T, -1):
                    ge(act, x2T_ps, G * q + g + 1)
                    ge(act, h2_ps, G * q + g - 1)
                    act.activation(x2T[:, g % 2], p_b[:, :], ACT.Copy).then_inc(x2T_ready, 1)
                for p in due_batch(b, t, PRE_ART_LN, 1):
                    ge(act, art_step, ART_STEPS * p + 7)
                    act.activation(art[:, 11], art[:, 7], ACT.Ln).then_inc(art_ln_done, 1)
                if live(b) and 2 <= t < SN + 2:
                    u = t - 2
                    ge(act, nt_ps, SN * b + u + 1)
                    act.activation(n_st[:, u % G, 0].rearrange("p c d -> p (c d)"), p_nt[:, :], ACT.Copy).then_inc(n_hi_ready, 1)
                for p, g in due(b, t, PRE_X1T, 1):
                    ge(act, x1T_ps, G * p + g + 1)
                    act.activation(h_first[:, g], p_a[:, :], ACT.Copy).then_inc(h_first_ready, 1)
                    act.activation(hh_first[:, g], p_a[:, :], ACT.Copy).then_inc(hh_first_ready, 1)
                for m, u in earlier(b, t, 2):
                    if u < SN:
                        ge(act, h_done, S * m + u + 1)
                        act.activation(hh_st[:, u % G], h_st[:, u % G], ACT.Copy).then_inc(hh_ready, 1)
                for p, g in due(b, t, PRE_MM, 1):
                    ge(act, sup_ps, G * p + g + 1)
                    act.activation(v1[:, g], p_a[:, :].rearrange("p (c d) -> p c d", c=C), ACT.Copy)\
                        .then_inc(sup_ready, 1)
                for p, g in due(b, t, PRE_IN, 1):
                    ge(act, adjT_ps, G * p + g + 1)
                    ge(act, adjT_mid_in[g], 16 * p)
                    act.activation(adjT_pre[:, g].rearrange("p c i -> p (c i)"), p_a[:, :], ACT.Copy)\
                        .then_inc(adjT_ready, 1)
                for q, g in due(b, t, POST_AGG_T, -1):
                    ge(act, h3T_ps, G * q + g + 1)
                    ge(act, conv_ps, G * q + g - 1)
                    act.activation(h3T[:, g % 2], p_a[:, :], ACT.Copy).then_inc(h3T_ready, 1)
                for q, g in due(b, t, POST_X2, -1):
                    ge(act, ln2_ready, G * q + g + 1)
                    apply(res, res, ln2, g, x2_ready)
                for p, g in due(b, t, PRE_X1, 1):
                    ge(act, ln1_ready, G * p + g + 1)
                    ge(act, x1_post_in[g], 16 * p)
                    apply(x1_pre, v1, ln1, g, x1_ready)
                for q, g in due(b, t, POST_AGG, -1):
                    ge(act, agg3_ps, G * q + g + 1)
                    act.activation(agg3[:, g % 2], p_b[:, :], ACT.Copy).then_inc(agg3_ready, 1)
                if live(b):
                    ge(act, gates_ps, 4 * (S * b + t) + 4)
                    ge(act, zd_done, S * b + t - 1)
                    act.activation(z_s[:, t % 2], p_z[:, :], ACT.Sigmoid, bias=bias_rz[:, 1:2], scale=down[:, 1:2])\
                        .then_inc(z_ready, 1)
                if live(b):
                    ge(act, t2_done, S * b + t + 1)
                    ge(act, h_done, S * b + t - 1)
                    act.activation(c_s[:, t % 2], t_s[:, t % 2], ACT.Tanh, bias=bi[:, 2:3], scale=down[:, 2:3])\
                        .then_inc(cand_ready, 1)
                for q, g in due(b, t, POST_X3, -1):
                    ge(act, ln3_ready, G * q + g + 1)
                    apply(res, res, ln3, g, x3_ready)
                for p in due_batch(b, t, PRE_BALL, 1):
                    ge(act, ball_norm, G * (p + 1))
                    act.activation(ball[:, 2], ball[:, 1], ACT.Tanh).then_inc(ball_tanh, 1)
                for p, g in due(b, t, PRE_SQ, 1):
                    ge(act, x_loaded[g], 16 * (p + 1))
                    ge(act, sumsq_done, G * p + g)
                    for c in range(C):
                        last = act.activation(act_junk[:, c], x_in[:, g, c], ACT.Square, accum_out=col(sumsq, g, c))
                    last.then_inc(sumsq_done, 1)
                for p, g in due(b, t, PRE_X1_HI, 1):
                    ge(act, x1_ready, G * p + g + 1)
                    act.activation(n_first[:, g, 0], x1_pre[:, g], ACT.Copy).then_inc(n_first_hi, 1)
                for p, g in due(b, t, PRE_SUPSQ, 1):
                    ge(act, sup_ready, G * p + g + 1)
                    ge(act, sup_sq_done, G * p + g)
                    for c in range(C):
                        last = act.activation(act_junk[:, c], v1[:, g, c], ACT.Square, accum_out=col(sup_sq, g, c))
                    last.then_inc(sup_sq_done, 1)
            run(act, slot, setup)

        @block.vector
        def _(dve):
            def setup(t):
                if t == SET_SCALE:
                    dve.wait_ge(s_w[2], 16)
                    dve.tensor_reduce(rowmax[:, :, 0], w_hh_n[:, :, :], AX.X, ALU.max, apply_absolute_value=True)\
                        .then_inc(s_set_dve, 1)
                    dve.wait_ge(s_set_act, SET_V)
                    dve.tensor_reduce(rowmax[:, :, 1], vT[:, :, :], AX.X, ALU.max, apply_absolute_value=True)\
                        .then_inc(s_set_dve, 1)
                    dve.wait_ge(s_set_dve, 2)
                    dve.tensor_tensor(rowmax[:, :, 2], rowmax[:, :, 0], rowmax[:, :, 1], ALU.max).then_inc(s_set_dve, 1)
                    dve.wait_ge(s_set_dve, 3)
                    dve.tensor_scalar(up[:, :], rowmax[:, :, 2], 2.0 ** -100, 2.0 ** 100, ALU.max, ALU.min).then_inc(s_set_dve, 1)
                    dve.wait_ge(s_set_dve, 4)
                    down_i, up_i = down[:, :].bitcast(I32), up[:, :].bitcast(I32)
                    dve.tensor_scalar(down_i, up_i, 0x7F800000, None, ALU.bitwise_and).then_inc(s_set_dve, 1)
                    dve.wait_ge(s_set_dve, 5)
                    dve.tensor_scalar(up_i, down_i, -1.0, float((254 + SCALE_EXP) << 23), ALU.mult, ALU.add).then_inc(s_set_dve, 1)
                    dve.wait_ge(s_set_dve, 6)
                    dve.tensor_scalar(down_i, up_i, -1.0, float(254 << 23), ALU.mult, ALU.add).then_inc(s_set_dve, 1)
                    for k in range(3):
                        dve.tensor_scalar(vT[:, k], vT[:, k], up[:, k:k + 1], None, ALU.mult).then_inc(s_set_dve, 1)
                        dve.tensor_scalar(w_hh_n[:, k], w_hh_n[:, k], up[:, k:k + 1], None, ALU.mult).then_inc(s_set_dve, 1)
                    dve.wait_ge(s_w[3], 16)
                    dve.wait_ge(s_w[4], 16)
                    dve.tensor_tensor(bias_rz[:, :], bi[:, :], bh[:, :], ALU.add).then_inc(s_set_dve, 1)
                    dve.tensor_tensor(bias_hn[:, :], bh[:, 2:3], up[:, 2:3], ALU.mult).then_inc(s_set_dve, 1)
                    for k, tile in ((8, w_rel_s), (9, w_root_s), (10, b_rel_row)):
                        dve.wait_ge(s_w[k], 16)
                        dve.tensor_scalar(tile[:, :], tile[:, :], 0.5, None, ALU.mult).then_inc(s_half, 1)
                l = t - SET_SPLIT
                if 0 <= l <= L:
                    dve.wait_ge(s_set_act, 10 + l)
                    hi, lo = (v_hi[:, l], v_lo[:, l]) if l < L else (u_hi[:, :, :], u_lo[:, :, :])
                    dve.tensor_tensor(lo, (p_hn, p_r)[l % 2][:, 0:3 * P].rearrange("p (k c) -> p k c", k=3), hi,
                                      ALU.subtract).then_inc(s_set_dve, 1)

            def bn(src, g, st, done, src_done, value):
                ge(dve, src_done, value)
                for c in range(C):
                    last = dve.bn_stats(st[:, C * g + c], src[:, g, c])
                last.then_inc(done, 1)

            def art_steps(p):
                k0 = ART_STEPS * p

                def ts(dst, src, wait, a, c_, oa, ob=ALU.bypass):
                    ge(dve, art_step, k0 + wait)
                    dve.tensor_scalar(dst, src, a, c_, oa, ob).then_inc(art_step, 1)

                def tt(dst, i0, i1, wait, op):
                    ge(dve, art_step, k0 + wait)
                    dve.tensor_tensor(dst, i0, i1, op).then_inc(art_step, 1)
                return k0, ts, tt

            def slot(b, t):
                n = S * b + t
                if live(b):
                    ge(dve, r_ready, n + 1)
                    dve.scalar_tensor_tensor(out=t_s[:, t % 2], in0=p_hn[:, :], scalar=bias_hn[:, 0:1],
                                             in1=r_s[:, t % 2], op0=ALU.add, op1=ALU.mult).then_inc(t_done, 1)
                for p, g in due(b, t, PRE_BALL_MAX, 1):
                    part = slice(C * g, C * g + C)
                    ge(dve, sup_sq_done, G * p + g + 1)
                    dve.tensor_scalar(ball[:, 0, part], sup_sq[:, part], TINY_SQ, None, ALU.max).then_inc(ball_max, 1)
                for q, g in due(b, t, POST_CONV, -1):
                    ge(dve, conv_ps, G * q + g + 1)
                    ge(dve, out_stored[g], 16 * q)
                    dve.tensor_tensor(v4[:, g], p_b[:, :].rearrange("p (c d) -> p c d", c=C), graphs(b_rel_row),
                                      ALU.add).then_inc(conv_done, 1)
                for m, u in following(b, t):
                    ge(dve, agg_hi_ready, S * m + u + 1)
                    dve.tensor_tensor(agg_lo[:, u % 2], p_agg[:, :], agg_hi[:, u % 2], ALU.subtract)\
                        .then_inc(agg_lo_ready, 1)
                for q in due_batch(b, t, POST_LN2, -1):
                    ln_dve(dve, st2, ln2, ln2_step, LN_STEPS, q, st2_done, x2_ready)
                if live(b):
                    ge(dve, gates_ps, 4 * n + 3)
                    ge(dve, t_done, n + 1)
                    dve.tensor_tensor(t_s[:, t % 2], p_in[:, :], t_s[:, t % 2], ALU.add).then_inc(t2_done, 1)
                for q in due_batch(b, t, POST_LN4, -1):
                    ln_dve(dve, st4, ln4, ln4_step, LN_STEPS, q, st4_done, out_ready, EPS / 4)
                if live(b) and 2 <= t < SN + 2:
                    u = t - 2
                    ge(dve, n_hi_ready, SN * b + u + 1)
                    dve.tensor_tensor(n_st[:, u % G, 1].rearrange("p c d -> p (c d)"), p_nt[:, :],
                                      n_st[:, u % G, 0].rearrange("p c d -> p (c d)"), ALU.subtract).then_inc(n_ready, 1)
                for m, u in earlier(b, t, 1):
                    ge(dve, z_ready, S * m + u + 1)
                    ge(dve, d_ready, S * m + u + 1)
                    dve.tensor_tensor(d_s[:, u % 2], z_s[:, u % 2], d_s[:, u % 2], ALU.mult).then_inc(zd_done, 1)
                    ge(dve, zd_done, S * m + u + 1)
                    if u < G:
                        ge(dve, hT_ps, G * (m - 1) + u + 1)
                    dve.tensor_tensor(h_st[:, u % G], c_s[:, u % 2], d_s[:, u % 2], ALU.add).then_inc(h_done, 1)
                for q, g in due(b, t, POST_H, -1):
                    ge(dve, h2_ps, G * q + g + 1)
                    ge(dve, y_ps, G * q + g - 1)
                    dve.tensor_tensor(h2[:, g % 2], p_b[:, :].rearrange("p (c d) -> p c d", c=C), graphs(b2_row), ALU.add)\
                        .then_inc(h2b_done, 1)
                for q, g in due(b, t, POST_Y, -1):
                    ge(dve, y_ps, G * q + g + 1)
                    for c in range(C):
                        last = dve.scalar_tensor_tensor(out=res[:, g, c], in0=p_a[:, P * c:P * c + P],
                                                        scalar=col(dinv_post, g, c), in1=res[:, g, c],
                                                        op0=ALU.mult, op1=ALU.add)
                    last.then_inc(v3_done, 1)
                for q, g in due(b, t, POST_H3, -1):
                    ge(dve, x3_ready, G * q + g + 1)
                    ge(dve, ln3_factor, G * q + g + 1)
                    ge(dve, agg3_ps, G * q + g - 1)
                    for c in range(C):
                        last = dve.scalar_tensor_tensor(out=h3[:, g % 2, c], in0=res[:, g, c], scalar=col(ln3[:, 10], g, c),
                                                        in1=gamma_row[:, :], op0=ALU.mult, op1=ALU.mult)
                    last.then_inc(h3g_done, 1)
                for q, g in due(b, t, POST_V2, -1):
                    ge(dve, hT_ps, G * q + g + 1)
                    ge(dve, mask_in, 16 * (q + 1))
                    ge(dve, x1_post_in[g], 16 * (q + 1))
                    for c in range(C):
                        last = dve.scalar_tensor_tensor(out=res[:, g, c], in0=p_b[:, P * c:P * c + P],
                                                        scalar=col(mask_post, g, c), in1=x1_post[:, g, c],
                                                        op0=ALU.mult, op1=ALU.add)
                    last.then_inc(v2_done, 1)
                for p, g in due(b, t, PRE_DEG, 1):
                    if g == 0:
                        ge(dve, dinv_pre_done, G * p)
                    ge(dve, adj_off_done, G * p + g + 1)
                    dve.tensor_reduce(degree[:, C * g:C * g + C], adj_off[:, g % 2], AX.X, ALU.add)\
                        .then_inc(degree_done, 1)
                for q in due_batch(b, t, POST_LN3, -1):
                    ge(dve, ln3_factor, G * q)
                    ln_dve(dve, st3, ln3, ln3_step, LN3_STEPS, q, st3_done, x3_ready)
                    k0 = LN3_STEPS * q
                    dve.tensor_scalar(ln3[:, VAR], ln3[:, 4], 1.0 / P, None, ALU.mult).then_inc(ln3_step, 1)
                    ge(dve, ln3_step, k0 + 7)
                    dve.reciprocal(ln3[:, 9], ln3[:, VAR_EPS]).then_inc(ln3_step, 1)
                    ge(dve, ln3_step, k0 + 9)
                    dve.tensor_tensor(ln3[:, 9], ln3[:, 9], ln3[:, VAR], ALU.mult).then_inc(ln3_step, 1)
                    ge(dve, ln3_step, k0 + 10)
                    dve.tensor_scalar(ln3[:, 9], ln3[:, 9], EPS, None, ALU.add).then_inc(ln3_step, 1)
                for p in due_batch(b, t, PRE_ART_END, 1):
                    k0, ts, tt = art_steps(p)
                    ge(dve, art_ln_done, p + 1)
                    ge(dve, art_step, k0 + 14)
                    dve.scalar_tensor_tensor(out=art[:, 5], in0=art[:, 11], scalar=0.5, in1=art[:, 6],
                                             op0=ALU.mult, op1=ALU.mult).then_inc(art_step, 1)
                    tt(art[:, 9], art[:, 9], art[:, 5], 15, ALU.subtract)
                    tt(art[:, 9], art[:, 9], art[:, 10], 16, ALU.mult)
                    tt(tan_scale[:, :], art[:, 9], art[:, 5], 17, ALU.add)
                for p in due_batch(b, t, PRE_ART_SERIES, 1):
                    k0, ts, tt = art_steps(p)
                    ge(dve, art_norm, G * (p + 1))
                    ts(art[:, 2], art[:, 1], 0, ATANH_MAX, None, ALU.min)
                    dve.reciprocal(art[:, 6], art[:, 1]).then_inc(art_step, 1)
                    ts(art[:, 4], art[:, 2], 1, -1.0, 1.0, ALU.mult, ALU.add)
                    ts(art[:, 3], art[:, 2], 1, 1.0, None, ALU.add)
                    ge(dve, art_step, k0 + 3)
                    dve.reciprocal(art[:, 5], art[:, 4]).then_inc(art_step, 1)
                    tt(art[:, 8], art[:, 2], art[:, 2], 1, ALU.mult)
                    tt(art[:, 7], art[:, 3], art[:, 5], 5, ALU.mult)
                    ts(art[:, 9], art[:, 8], 6, 1.0 / SERIES[0], None, ALU.mult)
                    ts(art[:, 10], art[:, 2], 1, SERIES_BELOW, None, ALU.is_lt)
                    for i, k in enumerate(SERIES[1:]):
                        ge(dve, art_step, k0 + (9 + i if i else 8))
                        dve.scalar_tensor_tensor(out=art[:, 9], in0=art[:, 9], scalar=1.0 / k, in1=art[:, 8],
                                                 op0=ALU.add, op1=ALU.mult).then_inc(art_step, 1)
                    ts(art[:, 9], art[:, 9], 13, 1.0, None, ALU.add)
                for q, g in due(b, t, POST_OUT, -1):
                    ge(dve, ln4_ready, G * q + g + 1)
                    for c in range(C):
                        last = dve.tensor_scalar(v4[:, g, c], v4[:, g, c], col(ln4[:, RSTD], g, c),
                                                 col(ln4[:, SHIFT], g, c), ALU.mult, ALU.add)
                    last.then_inc(out_ready, 1)
                for p in due_batch(b, t, PRE_BALL_END, 1):
                    k0 = BALL_STEPS * p
                    ge(dve, ball_norm, G * (p + 1))
                    dve.reciprocal(ball[:, 3], ball[:, 1]).then_inc(ball_step, 1)
                    ge(dve, ball_tanh, p + 1)
                    ge(dve, ball_step, k0 + 1)
                    dve.scalar_tensor_tensor(out=ball[:, 3], in0=ball[:, 2], scalar=BALL_MAX, in1=ball[:, 3],
                                             op0=ALU.min, op1=ALU.mult).then_inc(ball_step, 1)
                for q, g in due(b, t, POST_V4, -1):
                    ge(dve, conv_done, G * q + g + 1)
                    dve.scalar_tensor_tensor(out=v4[:, g], in0=v4[:, g], scalar=0.0, in1=res[:, g],
                                             op0=ALU.max, op1=ALU.add).then_inc(v4_done, 1)
                for p, g in due(b, t, PRE_V, 1):
                    ge(dve, ball_step, BALL_STEPS * (p + 1))
                    for c in range(C):
                        last = dve.scalar_tensor_tensor(out=v1[:, g, c], in0=v1[:, g, c], scalar=col(ball[:, 3], g, c),
                                                        in1=x_in[:, g, c], op0=ALU.mult, op1=ALU.add)
                    last.then_inc(v1_done, 1)
                for p, g in due(b, t, PRE_V_BN, 1):
                    bn(v1, g, st1, st1_done, v1_done, G * p + g + 1)
                for q, g in due(b, t, POST_V2_BN, -1):
                    bn(res, g, st2, st2_done, v2_done, G * q + g + 1)
                for p, g in due(b, t, PRE_NORM_MAX, 1):
                    part = slice(C * g, C * g + C)
                    ge(dve, sumsq_done, G * p + g + 1)
                    dve.tensor_scalar(art[:, 0, part], sumsq[:, part], TINY_SQ, None, ALU.max).then_inc(art_max, 1)
                for q, g in due(b, t, POST_Y_BN, -1):
                    bn(res, g, st3, st3_done, v3_done, G * q + g + 1)
                if t >= S - G and live(b + 1):
                    g = t - (S - G)
                    ge(dve, agg_ps, S * b + t + 1)
                    ge(dve, adj_loaded[g], 16 * (b + 2))
                    dve.tensor_scalar(linked[:, g], adj_in[:, g].rearrange("p c j -> p (c j)"), 0.0, None,
                                      ALU.not_equal).then_inc(linked_ready, 1)
                for q, g in due(b, t, POST_V4_BN, -1):
                    bn(v4, g, st4, st4_done, v4_done, G * q + g + 1)
                for p in due_batch(b, t, PRE_LN, 1):
                    ln_dve(dve, st1, ln1, ln1_step, LN_STEPS, p, st1_done, x1_ready)
                if t == DINV_MOVE:
                    if live(b - 1):
                        ge(dve, dinv_mid_done, b)
                        ge(dve, v3_done, G * (b - 1))
                        dve.tensor_copy(dinv_post[:, :], dinv_mid[:, :])\
                            .then_inc(dinv_post_done, 1)
                    if live(b):
                        ge(dve, dinv_pre_done, G * (b + 1))
                        ge(dve, dinv_post_done, b)
                        dve.tensor_copy(dinv_mid[:, :], dinv_pre[:, :])\
                            .then_inc(dinv_mid_done, 1)
            run(dve, slot, setup)

        @block.tensor
        def _(pe):
            def turn(dst, src, n, identity=ident):
                for k in range(n):
                    last = pe.transpose(dst[:, P * k:P * k + P], src(k), identity[:, :])
                return last

            pe.wait_ge(s_const, 6)

            def setup(t):
                if t == SET_TURN:
                    pe.wait_ge(s_w[0], 16)
                    turn(p_hn, lambda k: w_ih_n[:, k], 3).then_inc(s_set_pe, 1)
                    pe.wait_ge(s_w[1], 16)
                    turn(p_r, lambda k: weight_n[:, k], C).then_inc(s_set_pe, 1)
                    turn(p_in, lambda k: weight_n[:, C + k], L - C).then_inc(s_set_pe, 1)
                    pe.wait_ge(s_w[5], 16)
                    turn(p_z, lambda k: mask_n[:, :], 1).then_inc(s_set_pe, 1)
                    pe.wait_ge(s_w[6], 16)
                    pe.wait_ge(s_set_act, SET_MASK)
                    turn(p_z[:, P:2 * P], lambda k: w2_n[:, :], 1).then_inc(s_set_pe, 1)
                if t == SET_ROWS:
                    pe.wait_ge(s_set_act, SET_W2)
                    for k in range(3):
                        pe.matmul((p_hn, p_r, p_in)[k][:, :], w_ihT[:, k], weightT[:, 0:W], start=True, stop=True)\
                            .then_inc(s_set_pe, 1)
                    for k in range(3):
                        last = pe.matmul(p_agg[:, P * k:P * k + P], w_ihT[:, k], weightT[:, W:L * P], start=True, stop=True)
                    last.then_inc(s_set_pe, 1)
                l = t - SET_SPLIT
                if 0 <= l <= L:
                    if l == 0:
                        pe.wait_ge(s_set_dve, 13)
                    if l >= 2:
                        pe.wait_ge(s_set_dve, 15 + l - 1)
                    src = (lambda k: vT[:, k, P * l:P * l + P]) if l < L else (lambda k: w_hh_n[:, k])
                    turn((p_hn, p_r)[l % 2], src, 3).then_inc(s_set_pe, 1)
                if l == L + 1:
                    pe.wait_ge(s_set_dve, 15 + L + 1)
                    for k in range(7, 13):
                        pe.wait_ge(s_w[k], 16)
                    pe.wait_ge(s_half, 3)

            reader = {"a": None, "b": None}

            def claim(b, bank):
                if reader[bank]:
                    s, per, off, c = reader[bank]
                    ge(pe, s, per * (b + off) + c)

            def operand(b, bank, s, value):
                if not reader[bank] or reader[bank][0] is not s:
                    ge(pe, s, value)

            def read_by(b, bank, s, batch_off, g):
                reader[bank] = (s, G, batch_off, g + 1)

            def next_iteration():
                for k, v in reader.items():
                    if v:
                        reader[k] = (v[0], v[1], v[2] - 1, v[3])

            def split3(bank, hi, lo, xh, xl, start, stop, before_lo=None):
                pe.matmul(bank[:, :], hi, xh, start=start, stop=False)
                pe.matmul(bank[:, :], lo, xh, start=False, stop=False)
                if before_lo:
                    before_lo()
                return pe.matmul(bank[:, :], hi, xl, start=False, stop=stop)

            def off_of(first, g, ahead):
                return ahead - (first + g) // S

            def aggregate(b, t):
                g = t % G
                n_old = n_first if t < G else n_st
                if t < G:
                    ge(pe, n_first_lo, G * b + g + 1)
                    ge(pe, linked_ready, G * b + g + 1)
                else:
                    ge(pe, n_ready, SN * b + t - G + 1)
                ge(pe, agg_lo_ready, S * b + t)
                for c in range(C):
                    for part in range(2):
                        last = pe.matmul(p_agg[:, P * c:P * c + P], n_old[:, g, part, c], linked[:, g, P * c:P * c + P],
                                         start=(part == 0), stop=(part == 1))
                last.then_inc(agg_ps, 1)

            def slot(b, t):
                g0, l, n = t % G, t // G, S * b + t
                if live(b):
                    if l == 0:
                        ge(pe, hl_first_ready, G * b + g0 + 1)
                        hh, hl = hh_first[:, g0], hl_first[:, g0]
                    else:
                        ge(pe, hl_ready, SN * b + t - G + 1)
                        hh, hl = hh_st[:, g0], hl_st[:, g0]
                    ah, al = agg_hi[:, t % 2], agg_lo[:, t % 2]
                    ge(pe, t_done, n)
                    split3(p_hn, u_hi[:, 2], u_lo[:, 2], hh, hl, True, True).then_inc(gates_ps, 1)
                if live(b):
                    ge(pe, r_ready, n)
                    split3(p_r, u_hi[:, 0], u_lo[:, 0], hh, hl, True, False)
                    ge(pe, agg_hi_ready, n + 1)
                    split3(p_r, v_hi[:, l, 0], v_lo[:, l, 0], ah, al, False, True,
                           lambda: ge(pe, agg_lo_ready, n + 1)).then_inc(gates_ps, 1)
                for m, u in following(b, t):
                    aggregate(m, u)
                for p, g in due(b, t, PRE_MM, 1):
                    ge(pe, x_tan_ready, G * p + g + 1)
                    claim(b, "a")
                    for c in range(C):
                        last = pe.matmul(p_a[:, P * c:P * c + P], adjT_pre[:, g, c], x_tan[:, g % 2, c],
                                         start=True, stop=True)
                    last.then_inc(sup_ps, 1)
                    read_by(b, "a", sup_ready, off_of(PRE_MM, g, 1), g)
                for q, g in due(b, t, POST_X2T, -1):
                    ge(pe, x2_ready, G * q + g + 1)
                    claim(b, "b")
                    turn(p_b, lambda c: res[:, g, c], C).then_inc(x2T_ps, 1)
                    read_by(b, "b", x2T_ready, off_of(POST_X2T, g, -1), g)
                if live(b) and 2 <= t < SN + 2:
                    u = t - 2
                    ge(pe, h_done, S * b + u + 1)
                    ge(pe, n_ready, SN * b + u)
                    turn(p_nt, lambda c: h_st[:, u % G, P * c:P * c + P], C).then_inc(nt_ps, 1)
                for p, g in due(b, t, PRE_X1T, 1):
                    ge(pe, x1_ready, G * p + g + 1)
                    claim(b, "a")
                    turn(p_a, lambda c: x1_pre[:, g, c], C).then_inc(x1T_ps, 1)
                    read_by(b, "a", hh_first_ready, off_of(PRE_X1T, g, 1), g)
                for q, g in due(b, t, POST_CONV, -1):
                    ge(pe, h3T_ready, G * q + g + 1)
                    operand(b, "b", agg3_ready, G * q + g + 1)
                    claim(b, "b")
                    for c in range(C):
                        o = p_b[:, P * c:P * c + P]
                        pe.matmul(o, agg3[:, g % 2, P * c:P * c + P], w_rel_s[:, :], start=True, stop=False)
                        last = pe.matmul(o, h3T[:, g % 2, P * c:P * c + P], w_root_s[:, :], start=False, stop=True)
                    last.then_inc(conv_ps, 1)
                    read_by(b, "b", conv_done, off_of(POST_CONV, g, -1), g)
                if live(b):
                    ge(pe, t2_done, n)
                    split3(p_in, v_hi[:, l, 2], v_lo[:, l, 2], ah, al, True, True).then_inc(gates_ps, 1)
                    ge(pe, z_ready, n)
                    split3(p_z, u_hi[:, 1], u_lo[:, 1], hh, hl, True, False)
                    split3(p_z, v_hi[:, l, 1], v_lo[:, l, 1], ah, al, False, True).then_inc(gates_ps, 1)
                for p, g in due(b, t, PRE_IN, 1):
                    ge(pe, adj_loaded[g], 16 * (p + 1))
                    claim(b, "a")
                    turn(p_a, lambda c: adj_in[:, g, c], C).then_inc(adjT_ps, 1)
                    read_by(b, "a", adjT_ready, off_of(PRE_IN, g, 1), g)
                for q, g in due(b, t, POST_Y, -1):
                    ge(pe, h2s_ready, G * q + g + 1)
                    ge(pe, adjT_post_in[g], 16 * (q + 1))
                    claim(b, "a")
                    for c in range(C):
                        last = pe.matmul(p_a[:, P * c:P * c + P], adjT_post[:, g, c], h2[:, g % 2, c],
                                         start=True, stop=True)
                    last.then_inc(y_ps, 1)
                    read_by(b, "a", v3_done, off_of(POST_Y, g, -1), g)
                for q, g in due(b, t, POST_V2, -1):
                    ge(pe, h_done, S * q + S - G + g + 1)
                    claim(b, "b")
                    turn(p_b, lambda c: h_st[:, g, P * c:P * c + P], C).then_inc(hT_ps, 1)
                    read_by(b, "b", v2_done, off_of(POST_V2, g, -1), g)
                for q, g in due(b, t, POST_AGG_T, -1):
                    ge(pe, h3_ready, G * q + g + 1)
                    claim(b, "a")
                    turn(p_a, lambda c: h3[:, g % 2, c], C).then_inc(h3T_ps, 1)
                    read_by(b, "a", h3T_ready, off_of(POST_AGG_T, g, -1), g)
                for q, g in due(b, t, POST_AGG, -1):
                    ge(pe, h3_ready, G * q + g + 1)
                    claim(b, "b")
                    for c in range(C):
                        last = pe.matmul(p_b[:, P * c:P * c + P], h3[:, g % 2, c], adjT_post[:, g, c],
                                         start=True, stop=True)
                    last.then_inc(agg3_ps, 1)
                    read_by(b, "b", agg3_ready, off_of(POST_AGG, g, -1), g)
                for q, g in due(b, t, POST_H, -1):
                    operand(b, "b", x2T_ready, G * q + g + 1)
                    claim(b, "b")
                    for c in range(C):
                        last = pe.matmul(p_b[:, P * c:P * c + P], x2T[:, g % 2, P * c:P * c + P], w2T[:, :],
                                         start=True, stop=True)
                    last.then_inc(h2_ps, 1)
                    read_by(b, "b", h2b_done, off_of(POST_H, g, -1), g)
                if t == S - 1:
                    next_iteration()
            run(pe, slot, setup)


_INS = ['x', 'adj', 'nodemask', 'L1_gnn_weight', 'L1_gnn_w_ih', 'L1_gnn_w_hh', 'L1_gnn_b_ih', 'L1_gnn_b_hh',
        'L2_gnn_W', 'L2_gnn_b', 'L3_gnn_W_rel', 'L3_gnn_b_rel', 'L3_gnn_W_root', 'L3_gnn_ln_gamma', 'L3_gnn_ln_beta']
_OUTS = [((128, 128, 128), 'float32')]


def kernel(**inputs):
    import numpy as _np
    import concourse.bacc as _bacc
    from concourse import mybir as _mybir
    from concourse.bass_utils import run_bass_kernel_spmd as _run

    nc = _bacc.Bacc("TRN2", target_bir_lowering=False, num_devices=1)
    arrays, args = {}, []
    for name in _INS:
        a = _np.ascontiguousarray(inputs[name])
        arrays[f"in_{name}_dram"] = a
        args.append(nc.dram_tensor(f"in_{name}_dram", a.shape, _mybir.dt.from_np(a.dtype), kind="ExternalInput").ap())
    for i, (shape, dtype) in enumerate(_OUTS):
        dt = _mybir.dt.from_np(_np.dtype(dtype))
        args.append(nc.dram_tensor(f"out_{i}_dram", shape, dt, kind="ExternalOutput").ap())
    build(nc, *args)
    r = _run(nc, [arrays], core_ids=[0])
    got = tuple(r.results[0][f"out_{i}_dram"] for i in range(len(_OUTS)))
    return got[0]
```
